# Optimizing a Trainium2 kernel written in Bass

```python
import numpy as np
import jax
import jax.numpy as jnp

def _softmax(x, axis=-1):
    return jax.nn.softmax(x, axis=axis)

def _gelu(x):
    return jax.nn.gelu(x, approximate=True)

def _silu(x):
    return jax.nn.silu(x)

def _sigmoid(x):
    return jax.nn.sigmoid(x)

def _layernorm(x, axis=-1, eps=1e-05):
    m = jnp.mean(x, axis=axis, keepdims=True)
    v = jnp.var(x, axis=axis, keepdims=True)
    return (x - m) / jnp.sqrt(v + eps)

def _scatter_add(tgt, idx, src, axis=0):
    return tgt.at[idx].add(src)

def _segment_sum(src, seg, n):
    return jax.ops.segment_sum(src, seg, n)
kernel_name = 'mk_macaron_d1_jaxref_r8_e0917e'

def setup_inputs(seed: int=0):
    np.random.seed(seed)
    _w = jnp.asarray

    def _L0_attn_setup():
        import jax, jax.numpy as jnp
        import numpy as np
        EMBED_DIM = 128
        NUM_HEADS = 16
        HEAD_DIM = EMBED_DIM // NUM_HEADS
        R_QKV = 32
        R_OUT = 32
        B, T = (4, 256)
        key = jax.random.key(seed)
        k1, k2, k3, k4, k5 = jax.random.split(key, 5)
        s = 0.02
        return {'x': jax.random.normal(k1, (B, T, EMBED_DIM), dtype=jnp.float32), 'W_qkv_v': jax.random.normal(k2, (R_QKV, EMBED_DIM), dtype=jnp.float32) * s, 'W_qkv_u': jax.random.normal(k3, (3 * EMBED_DIM, R_QKV), dtype=jnp.float32) * s, 'W_o_v': jax.random.normal(k4, (R_OUT, EMBED_DIM), dtype=jnp.float32) * s, 'W_o_u': jax.random.normal(k5, (EMBED_DIM, R_OUT), dtype=jnp.float32) * s}
    _L0_attn_in = _L0_attn_setup()

    def _L0_ffn_setup():
        import jax, jax.numpy as jnp
        import numpy as np
        H = 128
        I = 256
        E = 32
        B, S = (4, 256)

        def _grouped_mm(a, w, group_sizes):
            return jax.lax.ragged_dot(a, w, group_sizes)

        def _swiglu(x, gw, uw, dw):
            return jax.nn.silu(x @ gw) * (x @ uw) @ dw
        key = jax.random.key(seed)
        ks = jax.random.split(key, 8)
        scale = 0.02
        inp = {'hidden_states': jax.random.normal(ks[0], (B, S, H), dtype=jnp.float32), 'gate_w': jax.random.normal(ks[1], (H, E), dtype=jnp.float32) * scale, 'shared_gate_w': jax.random.normal(ks[2], (H, I), dtype=jnp.float32) * scale, 'shared_up_w': jax.random.normal(ks[3], (H, I), dtype=jnp.float32) * scale, 'shared_down_w': jax.random.normal(ks[4], (I, H), dtype=jnp.float32) * scale, 'routed_gate_w': jax.random.normal(ks[5], (E, H, I), dtype=jnp.float32) * scale, 'routed_up_w': jax.random.normal(ks[6], (E, H, I), dtype=jnp.float32) * scale, 'routed_down_w': jax.random.normal(ks[7], (E, I, H), dtype=jnp.float32) * scale}
        return inp
    _L0_ffn_in = _L0_ffn_setup()
    _d = {'L0_attn_x': _L0_attn_in['x'], 'L0_attn_W_qkv_v': _L0_attn_in['W_qkv_v'], 'L0_attn_W_qkv_u': _L0_attn_in['W_qkv_u'], 'L0_attn_W_o_v': _L0_attn_in['W_o_v'], 'L0_attn_W_o_u': _L0_attn_in['W_o_u'], 'L0_ffn_gate_w': _L0_ffn_in['gate_w'], 'L0_ffn_shared_gate_w': _L0_ffn_in['shared_gate_w'], 'L0_ffn_shared_up_w': _L0_ffn_in['shared_up_w'], 'L0_ffn_shared_down_w': _L0_ffn_in['shared_down_w'], 'L0_ffn_routed_gate_w': _L0_ffn_in['routed_gate_w'], 'L0_ffn_routed_up_w': _L0_ffn_in['routed_up_w'], 'L0_ffn_routed_down_w': _L0_ffn_in['routed_down_w']}
    _x0 = _d['L0_attn_x']
    _d['L0_attn_x'] = jax.random.normal(jax.random.fold_in(jax.random.key(seed), 1), (2, 1024, 128), dtype=_x0.dtype)
    del _x0
    return _d

def reference(L0_attn_x, L0_attn_W_qkv_v, L0_attn_W_qkv_u, L0_attn_W_o_v, L0_attn_W_o_u, L0_ffn_gate_w, L0_ffn_shared_gate_w, L0_ffn_shared_up_w, L0_ffn_shared_down_w, L0_ffn_routed_gate_w, L0_ffn_routed_up_w, L0_ffn_routed_down_w):

    def _L0_attn_ref(x, W_qkv_v, W_qkv_u, W_o_v, W_o_u):
        import jax, jax.numpy as jnp
        import numpy as np
        EMBED_DIM = 128
        NUM_HEADS = 16
        HEAD_DIM = EMBED_DIM // NUM_HEADS
        R_QKV = 32
        R_OUT = 32
        B, T = (4, 256)
        Bq, Tq, C = x.shape
        H, D = (NUM_HEADS, HEAD_DIM)
        qkv = x @ W_qkv_v.T @ W_qkv_u.T
        q, k, v = jnp.split(qkv, 3, axis=-1)
        q = q.reshape(Bq, Tq, H, D).transpose(0, 2, 1, 3)
        k = k.reshape(Bq, Tq, H, D).transpose(0, 2, 1, 3)
        v = v.reshape(Bq, Tq, H, D).transpose(0, 2, 1, 3)
        scale = 1.0 / jnp.sqrt(jnp.asarray(D, dtype=x.dtype))
        scores = jnp.einsum('bhtd,bhsd->bhts', q, k) * scale
        attn = jax.nn.softmax(scores.astype(jnp.float32), axis=-1).astype(q.dtype)
        y = jnp.einsum('bhts,bhsd->bhtd', attn, v)
        y = y.transpose(0, 2, 1, 3).reshape(Bq, Tq, C)
        y = y @ W_o_v.T @ W_o_u.T
        return y

    def _L0_ffn_ref(hidden_states, gate_w, shared_gate_w, shared_up_w, shared_down_w, routed_gate_w, routed_up_w, routed_down_w):
        import jax, jax.numpy as jnp
        import numpy as np
        H = 128
        I = 256
        E = 32
        B, S = (4, 256)

        def _grouped_mm(a, w, group_sizes):
            return jax.lax.ragged_dot(a, w, group_sizes)

        def _swiglu(x, gw, uw, dw):
            return jax.nn.silu(x @ gw) * (x @ uw) @ dw
        b, s, h = hidden_states.shape
        x = hidden_states.reshape(-1, h)
        shared_out = _swiglu(x, shared_gate_w, shared_up_w, shared_down_w)
        logits = x @ gate_w
        topk_ids = jnp.argmax(logits, axis=-1)
        topk_val = jnp.max(logits, axis=-1)
        scores = jax.nn.sigmoid(topk_val)[:, None]
        xs = x * scores
        tokens_per_expert = jnp.zeros((E,), jnp.int32).at[topk_ids].add(1)
        order = jnp.argsort(topk_ids)
        sorted_x = xs[order]
        g = _grouped_mm(sorted_x, routed_gate_w, tokens_per_expert)
        u = _grouped_mm(sorted_x, routed_up_w, tokens_per_expert)
        d = _grouped_mm(jax.nn.silu(g) * u, routed_down_w, tokens_per_expert)
        inv = jnp.argsort(order)
        routed_out = d[inv]
        return (shared_out + routed_out).reshape(b, s, h)
    x = L0_attn_x
    x = x + 0.5 * _L0_ffn_ref(_layernorm(x, axis=-1), L0_ffn_gate_w, L0_ffn_shared_gate_w, L0_ffn_shared_up_w, L0_ffn_shared_down_w, L0_ffn_routed_gate_w, L0_ffn_routed_up_w, L0_ffn_routed_down_w)
    x = x + _L0_attn_ref(_layernorm(x, axis=-1), L0_attn_W_qkv_v, L0_attn_W_qkv_u, L0_attn_W_o_v, L0_attn_W_o_u)
    x = x + 0.5 * _L0_ffn_ref(_layernorm(x, axis=-1), L0_ffn_gate_w, L0_ffn_shared_gate_w, L0_ffn_shared_up_w, L0_ffn_shared_down_w, L0_ffn_routed_gate_w, L0_ffn_routed_up_w, L0_ffn_routed_down_w)
    return x

_drawn_inputs = setup_inputs


def setup_inputs(seed=0):
    import zlib

    import numpy as np

    out = dict(_drawn_inputs(seed))
    spreads = {}
    factors = {'L0_attn_W_qkv_v': 8.0,
     'L0_attn_W_qkv_u': 8.0,
     'L0_attn_W_o_v': 8.0,
     'L0_attn_W_o_u': 8.0,
     'L0_ffn_gate_w': 8.0,
     'L0_ffn_shared_gate_w': 6.816,
     'L0_ffn_shared_up_w': 6.749,
     'L0_ffn_shared_down_w': 6.816,
     'L0_ffn_routed_gate_w': 8.0,
     'L0_ffn_routed_up_w': 8.0,
     'L0_ffn_routed_down_w': 8.0}
    for name, (base, spread) in spreads.items():
        noise = np.random.default_rng([zlib.crc32(name.encode()), seed]).standard_normal(out[name].shape)
        drawn = base * np.exp(spread * noise) if base else spread * noise
        out[name] = jnp.asarray(drawn.astype(out[name].dtype))
    for name, factor in factors.items():
        out[name] = (out[name] * factor).astype(out[name].dtype)
    return out
```

```python
from contextlib import ExitStack

import concourse.bass as bass
from concourse import mybir

F32 = mybir.dt.float32
BF16 = mybir.dt.bfloat16
I32 = mybir.dt.int32
U32 = mybir.dt.uint32
ALU = mybir.AluOpType
ACT = mybir.ActivationFunctionType
AX_X = mybir.AxisListType.X

P = 128
BANK = 512
TILES = 16
QUADS = TILES // 4
TOKENS = TILES * P
EXPERTS = 32
INNER = 256
WROW = 3 * INNER
SLOT_TILES = 48
ROW = P + 4
NOWHERE = 4 * TOKENS
EPS = 1e-5

HEADS = 16
HD = 8
SEQ = 1024
GH = 4
GROUPS = 2 * HEADS // GH
UNITS = 2 * GROUPS
CHUNKS = SEQ // P
QW = 512
STEPS = CHUNKS * GH
AHEAD = 6
MBLOCKS = GH * QW // P
Q_PARTS = (0, 0, 1, 1, 0, 2)
K_PARTS = (0, 1, 0, 1, 2, 0)
MROW = 96
SCALE = float(HD) ** -0.5


class Tally:

    def __init__(self, sem):
        self.sem, self.base, self.n = sem, 0, 0

    def done(self, ins):
        ins.then_inc(self.sem, 1)
        self.n += 1
        return self.base + self.n


def at_least(eng, sem, value):
    if not isinstance(value, int) or value > 0:
        eng.wait_ge(sem, value)


def build(nc, x_in, w_qkv_v, w_qkv_ut, w_o_v, w_o_ut, gate_w, sh_gate, sh_up, sh_down, r_gate, r_up, r_down, out):
    x_view = x_in.rearrange("b (t p) h -> p (b t) h", p=P)
    out_view = out.rearrange("b (t p) h -> p (b t) h", p=P)

    with ExitStack() as ctx:
        def sb(name, shape, dt=F32):
            return ctx.enter_context(nc.sbuf_tensor(name, shape, dt))

        def sem(name):
            return ctx.enter_context(nc.semaphore(name))

        rows_dram = [nc.dram_tensor(f"rows{n}", (SLOT_TILES * P, ROW), F32, kind="Internal").ap() for n in range(2)]
        y_dram = [nc.dram_tensor(f"y{n}", (TOKENS, P), F32, kind="Internal").ap() for n in range(2)]
        parts_dram = nc.dram_tensor("parts", (2, 3, 2 * P, SEQ), BF16, kind="Internal").ap()

        pair = [ctx.enter_context(nc.psum_tensor(f"pair{i}", [P, 2 * BANK], F32)) for i in range(2)]
        bank = [pair[i // 2][:, i % 2 * BANK:(i % 2 + 1) * BANK] for i in range(4)]
        bank += [ctx.enter_context(nc.psum_tensor(f"bank{i}", [P, BANK], F32))[:, :] for i in range(4, 8)]

        w_exp = sb("w_exp", [P, EXPERTS * WROW])
        w_sh = sb("w_sh", [P, WROW])
        gate_sb = sb("gate_sb", [P, EXPERTS])
        wv_sb = sb("wv_sb", [32, P])
        wut_sb = sb("wut_sb", [32, 3 * P])
        wov_sb = sb("wov_sb", [32, P])
        wout_sb = sb("wout_sb", [32, P])
        w_qkv = sb("w_qkv", [P, 3 * P])
        w_out = sb("w_out", [P, P])

        xres = sb("xres", [P, TILES, P])
        xn = sb("xn", [P, TILES, ROW])
        xnT = sb("xnT", [P, TOKENS])
        y_back = xnT[:, :].rearrange("p (t h) -> p t h", h=P)

        identf = sb("identf", [P, P])
        identb = sb("identb", [P, P], BF16)
        before = sb("before", [P, P], BF16)
        onesb = sb("onesb", [P, P], BF16)
        iota_i = sb("iota_i", [P, EXPERTS], I32)
        rev = sb("rev", [P, EXPERTS])
        slot_tile_i = sb("slot_tile_i", [P, 1], I32)
        slot_tile = sb("slot_tile", [P, 1])
        zeros = sb("zeros", [P, EXPERTS])
        empty_row = sb("empty_row", [P, ROW])

        stats = sb("stats", [P, TILES, 6])
        mv = sb("mv", [P, TILES, 2])
        var = sb("var", [P, TILES])
        std = sb("std", [P, TILES])
        rstd = sb("rstd", [P, TILES])
        newton = sb("newton", [P, 4])
        top = sb("top", [P, TILES])
        rtop = sb("rtop", [P, TILES])
        escore = sb("escore", [P, TILES])
        score = sb("score", [P, TILES])
        count_i = sb("count_i", [P, EXPERTS], I32)
        slots_of = sb("slots_of", [P, EXPERTS])
        slots_to = sb("slots_to", [P, EXPERTS])
        base_e = sb("base_e", [P, EXPERTS])
        below = sb("below", [P, EXPERTS])
        eid = sb("eid", [P, 1])
        slot_f = sb("slot_f", [P, TILES])
        slot_i = sb("slot_i", [P, TILES], I32)
        woff = sb("woff", [1, P], I32)

        xe = [sb(f"xe{i}", [P, ROW]) for i in range(4)]
        xeT = [sb(f"xeT{i}", [P, P]) for i in range(2)]
        yb = [sb(f"yb{i}", [P, P]) for i in range(4)]
        slot_token = sb("slot_token", [P, 8], I32)

        arena = sb("arena", [P, 8 * BANK])
        silu_sb = [arena[:, i * BANK:(i + 1) * BANK] for i in range(2)]
        h_sh = [[arena[:, (2 + 2 * i + c) * BANK:(3 + 2 * i + c) * BANK] for c in range(2)] for i in range(2)]
        h_sb = [arena[:, 6 * BANK + i * INNER:6 * BANK + (i + 1) * INNER] for i in range(2)]
        hT_sb = [arena[:, 7 * BANK + i * INNER:7 * BANK + (i + 1) * INNER] for i in range(2)]
        part_sb = [arena[:, i * 768:(i + 1) * 768].bitcast(BF16).rearrange("p (c t) -> p c t", c=3) for i in range(2)]
        rest_sb = [arena[:, (3 + i) * BANK:(4 + i) * BANK] for i in range(2)]
        prob = [arena[:, i * BANK:(i + 1) * BANK] for i in range(8)]

        arena2 = sb("arena2", [P, 2, CHUNKS, GH, 32])
        flat2 = arena2[:, :, :, :, :].rearrange("p a c h d -> p (a c h d)")
        hit = flat2[:, 0:512].rearrange("p (t e) -> p t e", e=EXPERTS)
        cand = flat2[:, 512:1024].rearrange("p (t e) -> p t e", e=EXPERTS)
        place = flat2[:, 1024:1536].rearrange("p (t e) -> p t e", e=EXPERTS)
        onehot = flat2[:, 1536:1792].bitcast(BF16)
        onehot3 = onehot.rearrange("p (t e) -> p t e", e=EXPERTS)
        v_grp = [arena2[:, i] for i in range(2)]

        v_all = sb("v_all", [P, GROUPS, CHUNKS * GH * (HD + 1)])
        v_all5 = v_all[:, :, :].rearrange("p g (c h d) -> p g c h d", c=CHUNKS, h=GH)
        q_stack = [sb(f"q_stack{i}", [P, 2, GH, QW], BF16) for i in range(2)]
        k_stack = [sb(f"k_stack{i}", [P, GH, SEQ], BF16) for i in range(2)]
        rowmax = [sb(f"rowmax{i}", [P, MBLOCKS]) for i in range(2)]
        mrest = sb("mrest", [P, MBLOCKS])
        mpart = sb("mpart", [P, P // MBLOCKS, MBLOCKS], BF16)
        mT = sb("mT", [3 * MBLOCKS, P], BF16)
        oT = sb("oT", [P, QW])
        rden = sb("rden", [P, 4, GH])

        x_loaded = [sem(f"x_loaded{g}") for g in range(QUADS)]
        small_loaded = sem("small_loaded")
        experts_loaded = sem("experts_loaded")
        consts_ready = sem("consts_ready")
        stacks_cleared = sem("stacks_cleared")
        prefilled = [sem(f"prefilled{n}") for n in range(2)]
        weights_ps = sem("weights_ps")
        weights_sb = sem("weights_sb")
        dve_own = sem("dve_own")
        pool_own = sem("pool_own")
        var_ready = sem("var_ready")
        std_ready = sem("std_ready")
        xn_ready = sem("xn_ready")
        xnT_ps = sem("xnT_ps")
        xnT_ready = sem("xnT_ready")
        logits_ready = sem("logits_ready")
        top_ready = sem("top_ready")
        escore_ready = sem("escore_ready")
        onehot_ready = sem("onehot_ready")
        ranks_ready = sem("ranks_ready")
        eid_ready = sem("eid_ready")
        eid_row = sem("eid_row")
        woff_ready = sem("woff_ready")
        slots_ready = sem("slots_ready")
        scattered = sem("scattered")
        shg_ps = sem("shg_ps")
        shsilu_sb = sem("shsilu_sb")
        shh_sb = sem("shh_sb")
        shy_ps = sem("shy_ps")
        shy_added = sem("shy_added")
        xe_loaded = [sem(f"xe_loaded{i}") for i in range(4)]
        xeT_ps = sem("xeT_ps")
        xeT_sb = sem("xeT_sb")
        gu_ps = sem("gu_ps")
        silu_done = sem("silu_done")
        h_done = sem("h_done")
        hT_ps = sem("hT_ps")
        hT_done = sem("hT_done")
        y_ps = sem("y_ps")
        y_done = sem("y_done")
        ids_done = sem("ids_done")
        y_stored = [sem(f"y_stored{i}") for i in range(4)]
        stores_begun = sem("stores_begun")
        y_loaded = [sem(f"y_loaded{g}") for g in range(QUADS)]
        qk_ps = sem("qk_ps")
        part0_sb = sem("part0_sb")
        rest_ready = sem("rest_ready")
        part1_sb = sem("part1_sb")
        part2_sb = sem("part2_sb")
        parts_stored = [sem(f"parts_stored{i}") for i in range(2)]
        v_ps = sem("v_ps")
        v_sb = sem("v_sb")
        stack_loaded = [sem(f"stack_loaded{i}") for i in range(2)]
        vgrp_ready = sem("vgrp_ready")
        smax_ps = sem("smax_ps")
        smax_read = sem("smax_read")
        mparts_ready = sem("mparts_ready")
        mT_ps = sem("mT_ps")
        mT_ready = sem("mT_ready")
        m_loaded = [sem(f"m_loaded{i}") for i in range(2)]
        score_ps = sem("score_ps")
        prob_ready = sem("prob_ready")
        pv_done = sem("pv_done")
        oT_ready = sem("oT_ready")
        o_ps = sem("o_ps")
        o_normed = sem("o_normed")
        yT_ps = sem("yT_ps")
        yT_ready = sem("yT_ready")
        proj_ps = sem("proj_ps")
        stored = sem("stored")

        xn_tile = lambda t: xn[:, t, 0:P]
        quad = lambda g: slice(4 * g, 4 * g + 4)

        block = ctx.enter_context(nc.Block())

        @block.sync
        def _(sp):
            for g in range(QUADS):
                sp.dma_start(xres[:, quad(g), :], x_view[:, quad(g), :]).then_inc(x_loaded[g], 16)
            for dst, src in ((gate_sb[:, :], gate_w), (w_sh[:, 0:INNER], sh_gate), (w_sh[:, INNER:2 * INNER], sh_up),
                             (w_sh[:, 2 * INNER:].rearrange("p (c h) -> p c h", c=2), sh_down.rearrange("(c p) h -> p c h", p=P)),
                             (wv_sb[:, :], w_qkv_v), (wut_sb[:, :], w_qkv_ut), (wov_sb[:, :], w_o_v), (wout_sb[:, :], w_o_ut)):
                sp.dma_start(dst, src).then_inc(small_loaded, 16)
            sp.wait_ge(consts_ready, 1)

            def prefill(n):
                sp.dma_start(rows_dram[n].rearrange("(j p) r -> p j r", p=P),
                             empty_row[:, :].unsqueeze(1).broadcast_to([P, SLOT_TILES, ROW])).then_inc(prefilled[n], 16)

            prefill(0)
            w3 = w_exp[:, :].rearrange("p (e w) -> p e w", w=WROW)
            step = EXPERTS // 4
            for e in range(0, EXPERTS, step):
                sp.dma_start(w3[:, e:e + step, 0:INNER], r_gate[e:e + step].rearrange("e h i -> h e i")).then_inc(experts_loaded, 16)
                sp.dma_start(w3[:, e:e + step, INNER:2 * INNER], r_up[e:e + step].rearrange("e h i -> h e i")).then_inc(experts_loaded, 16)
                for c in range(2):
                    sp.dma_start(w3[:, e:e + step, 2 * INNER + c * P:2 * INNER + (c + 1) * P],
                                 r_down[e:e + step, c * P:(c + 1) * P, :].rearrange("e p h -> p e h")).then_inc(experts_loaded, 16)
            prefill(1)

            def ffn(n):
                sp.wait_ge(scattered, 16 * TILES * (n + 1))

                def load(j, r):
                    at_least(sp, xeT_ps, n * SLOT_TILES + j - 3)
                    at_least(sp, ids_done, n * SLOT_TILES + j - 3)
                    sp.dma_start(xe[r][:, :], rows_dram[n][bass.ds(j * P, P), :]).then_inc(xe_loaded[r], 16)

                for r in range(4):
                    load(r, r)
                with sp.Fori(1, SLOT_TILES // 4) as k:
                    for r in range(4):
                        load(4 * k + r, r)
                for i in range(4):
                    sp.wait_ge(y_stored[i], 4 * SLOT_TILES * (n + 1))
                y_view = y_dram[n].rearrange("(t p) h -> p t h", p=P)
                for g in range(QUADS):
                    sp.dma_start(y_back[:, quad(g), :], y_view[:, quad(g), :]).then_inc(y_loaded[g], 16)

            def attention():
                for i in range(8):
                    b, qk, half = i // 4, i // 2 % 2, i % 2
                    sp.wait_ge(part2_sb, i + 1)
                    sp.dma_start(parts_dram[qk, :, b * P:(b + 1) * P, half * BANK:(half + 1) * BANK].rearrange("c p t -> p c t"),
                                 part_sb[i % 2]).then_inc(parts_stored[i % 2], 16)

                def load_stacks(g, r):
                    for term in range(len(Q_PARTS)):
                        rows = slice(term * HD, (term + 1) * HD)
                        src = [parts_dram[qk, part, bass.ds(g * GH * HD, GH * HD), :].rearrange("(h d) t -> d h t", d=HD)
                               for qk, part in enumerate((Q_PARTS[term], K_PARTS[term]))]
                        for half in range(2):
                            sp.dma_start(q_stack[r][rows, half, :, :], src[0][:, :, half * QW:(half + 1) * QW]).then_inc(stack_loaded[r], 16)
                        sp.dma_start(k_stack[r][rows, :, :], src[1]).then_inc(stack_loaded[r], 16)

                def load_m(u):
                    half, r = u[1] % 2, u[1] // 2 % 2
                    sp.wait_ge(mT_ready, u[0] + 1)
                    for c in range(3):
                        dst = q_stack[r][MROW + c:MROW + c + 1, half, :, :].rearrange("o h t -> o (h t)")
                        src = mT[c * MBLOCKS:(c + 1) * MBLOCKS, :]
                        sp.dma_start(dst, src).then_inc(m_loaded[half], 16)

                sp.wait_ge(stacks_cleared, 1)
                for i in range(2):
                    sp.wait_ge(parts_stored[i], 32)
                load_stacks(0, 0)
                load_stacks(1, 1)
                for i in range(2):
                    sp.wait_ge(parts_stored[i], 64)
                load_m((0, 0))
                with sp.Fori(0, GROUPS // 2 - 1) as k:
                    for s in range(4):
                        load_m((4 * k + s + 1, s + 1))
                        if s % 2:
                            sp.wait_ge(pv_done, CHUNKS * (4 * k + s + 1))
                            load_stacks(2 * k + s // 2 + 2, s // 2)
                for s in range(3):
                    load_m((UNITS - 4 + s + 1, s + 1))

            ffn(0)
            attention()
            ffn(1)
            for g in range(QUADS):
                sp.wait_ge(xn_ready, 3 * QUADS + g + 1)
                sp.dma_start(out_view[:, quad(g), :], xres[:, quad(g), :]).then_inc(stored, 16)
            sp.wait_ge(stored, 16 * QUADS)

        @block.gpsimd
        def _(pool):
            own = Tally(pool_own)
            nc.gpsimd.memset(empty_row[:, 0:P], 0.0)
            nc.gpsimd.memset(empty_row[:, P:ROW].bitcast(I32), NOWHERE).then_inc(consts_ready, 1)
            nc.gpsimd.memset(identf[:, :], 0.0)
            nc.gpsimd.memset(identb[:, :], 0.0)
            nc.gpsimd.memset(before[:, :], 1.0)
            nc.gpsimd.memset(onesb[:, :], 1.0)
            nc.gpsimd.memset(zeros[:, :], 0.0)
            nc.gpsimd.iota(xn[:, :, P:ROW].bitcast(I32), pattern=[[P, TILES], [0, 4]], base=0, channel_multiplier=1)
            nc.gpsimd.iota(slot_tile_i[:, :], pattern=[[0, 1]], base=0, channel_multiplier=1)
            w = own.done(nc.gpsimd.iota(iota_i[:, :], pattern=[[-1, EXPERTS]], base=EXPERTS, channel_multiplier=0))
            pool.wait_ge(pool_own, w)
            nc.gpsimd.affine_select(out=identf[:, :], in_=identf[:, :], compare_op=ALU.not_equal, fill=1.0,
                                    base=0, pattern=[[-1, P]], channel_multiplier=1)
            nc.gpsimd.affine_select(out=identb[:, :], in_=identb[:, :], compare_op=ALU.not_equal, fill=1.0,
                                    base=0, pattern=[[-1, P]], channel_multiplier=1)
            nc.gpsimd.affine_select(out=before[:, :], in_=before[:, :], compare_op=ALU.is_gt, fill=0.0,
                                    base=0, pattern=[[1, P]], channel_multiplier=-1)
            nc.gpsimd.tensor_copy(slot_tile[:, :], slot_tile_i[:, :])
            nc.gpsimd.tensor_copy(rev[:, :], iota_i[:, :]).then_inc(consts_ready, 1)
            for i in range(2):
                nc.gpsimd.memset(q_stack[i][:, :, :, :].bitcast(F32), 0.0)
                nc.gpsimd.memset(k_stack[i][0:MROW, :, :].bitcast(F32), 0.0)
            pool.wait_ge(pool_own, own.done(nc.gpsimd.memset(v_all[:, :, :], 1.0)))
            for i in range(2):
                w = own.done(nc.gpsimd.memset(k_stack[i][MROW:P, :, :], 1.0))
            pool.wait_ge(pool_own, w)
            pool.sem_inc(stacks_cleared, 1)

            def ffn(n):
                pool.wait_ge(prefilled[n], 16)
                pool.wait_ge(slots_ready, n + 1)
                for t in range(TILES):
                    nc.gpsimd.indirect_dma_start(
                        rows_dram[n], bass.IndirectOffsetOnAxis(slot_i[:, t:t + 1].bitcast(U32), 0),
                        xn[:, t, :], None).then_inc(scattered, 16)

                def store(j, r):
                    pool.wait_ge(y_done, n * SLOT_TILES + j + 1)
                    pool.sem_inc(stores_begun, 1)
                    nc.gpsimd.indirect_dma_start(
                        y_dram[n], bass.IndirectOffsetOnAxis(slot_token[:, r:r + 1].bitcast(U32), 0),
                        yb[r % 4][:, :], None, bounds_check=TOKENS - 1, oob_is_err=False).then_inc(y_stored[r % 4], 16)

                with pool.Fori(0, SLOT_TILES // 8) as k:
                    for r in range(8):
                        store(8 * k + r, r)

            def attention():
                pool.wait_ge(xn_ready, QUADS + 1)
                nc.gpsimd.memset(mpart[:, :, :], 0.0)
                for i in range(2):
                    last = nc.gpsimd.memset(arena2[:, i], 0.0)
                pool.wait_ge(pool_own, own.done(last))

                def values(g, r):
                    src = v_all[:, bass.ds(g, 1), :].rearrange("p o (c h d) -> p (o c) h d", c=CHUNKS, h=GH)
                    nc.gpsimd.tensor_copy(v_grp[r][:, :, :, 0:HD + 1], src).then_inc(vgrp_ready, 1)

                def m_parts(u, half):
                    pool.wait_ge(smax_read, MBLOCKS * (u + 1))
                    at_least(pool, mT_ps, u)
                    m = rowmax[half][:, :]
                    zero = zeros[:, 0:MBLOCKS]
                    pool.wait_ge(pool_own, own.done(nc.gpsimd.tensor_tensor(mpart[:, 0, :], zero, m, ALU.subtract)))
                    pool.wait_ge(pool_own, own.done(nc.gpsimd.tensor_tensor(mrest[:, :], m, mpart[:, 0, :], ALU.add)))
                    pool.wait_ge(pool_own, own.done(nc.gpsimd.tensor_tensor(mpart[:, 1, :], zero, mrest[:, :], ALU.subtract)))
                    pool.wait_ge(pool_own, own.done(nc.gpsimd.tensor_tensor(mrest[:, :], mrest[:, :], mpart[:, 1, :], ALU.add)))
                    nc.gpsimd.tensor_tensor(mpart[:, 2, :], zero, mrest[:, :], ALU.subtract).then_inc(mparts_ready, 1)

                pool.wait_ge(v_sb, 4)
                values(0, 0)
                values(1, 1)
                m_parts(0, 0)
                per = 16
                start = own.n
                with pool.Fori(0, GROUPS // 2 - 1) as k:
                    own.base, own.n = start + k * per, 0
                    for s in range(4):
                        m_parts(4 * k + s + 1, (s + 1) % 2)
                        if s % 2:
                            pool.wait_ge(pv_done, 8 * (4 * k + s + 1))
                            values(2 * k + s // 2 + 2, s // 2)
                    assert own.n == per
                own.base, own.n = 0, start + per * (GROUPS // 2 - 1)
                for s in range(3):
                    m_parts(UNITS - 4 + s + 1, (s + 1) % 2)

            ffn(0)
            attention()
            ffn(1)

        @block.scalar
        def _(act):
            def transposed(use):
                for g in range(QUADS):
                    act.wait_ge(var_ready, use * QUADS + g + 1)
                    nc.scalar.activation(std[:, quad(g)], var[:, quad(g)], ACT.Sqrt).then_inc(std_ready, 1)
                for g in range(QUADS):
                    act.wait_ge(xnT_ps, use * QUADS + g + 1)
                    nc.scalar.activation(xnT[:, g * BANK:(g + 1) * BANK], bank[g % 2], ACT.Copy).then_inc(xnT_ready, 1)

            def ffn(n):
                transposed(2 * n)
                act.wait_ge(top_ready, n + 1)
                nc.scalar.activation(escore[:, :], top[:, :], ACT.Exp, scale=-1.0).then_inc(escore_ready, 1)
                for i in range(2 * QUADS):
                    act.wait_ge(shg_ps, 8 * n + i + 1)
                    at_least(act, shh_sb, 8 * n + i - 1)
                    nc.scalar.activation(silu_sb[i % 2], bank[5 * (i % 2)][:, :], ACT.Silu).then_inc(shsilu_sb, 1)

                base = n * SLOT_TILES

                def x_out(j, r):
                    act.wait_ge(xeT_ps, base + j + 1)
                    at_least(act, gu_ps, base + j - 1)
                    nc.scalar.activation(xeT[r % 2][:, :], bank[5 + r % 2][:, 0:P], ACT.Copy).then_inc(xeT_sb, 1)

                def silu(j, r):
                    act.wait_ge(gu_ps, base + j + 1)
                    at_least(act, h_done, base + j - 1)
                    nc.scalar.activation(silu_sb[r % 2][:, 0:INNER], bank[r % 2][:, 0:INNER], ACT.Silu).then_inc(silu_done, 1)

                def y_out(j, r):
                    act.wait_ge(y_ps, base + j + 1)
                    at_least(act, y_stored[r % 4], 4 * (base + j - r % 4))
                    nc.scalar.activation(yb[r % 4][:, :], bank[(4, 7)[r % 2]][:, 0:P], ACT.Copy).then_inc(y_done, 1)

                act.wait_ge(shh_sb, 8 * (n + 1))
                x_out(0, 0)

                def turn(j, r):
                    if not isinstance(j, int) or j + 1 < SLOT_TILES:
                        x_out(j + 1, r + 1)
                    silu(j, r)
                    if not isinstance(j, int) or j >= 3:
                        y_out(j - 3, r + 5)

                for j in range(8):
                    turn(j, j)
                with act.Fori(1, SLOT_TILES // 8 - 1) as k:
                    for r in range(8):
                        turn(8 * k + r, r)
                for j in range(SLOT_TILES - 8, SLOT_TILES):
                    turn(j, j)
                for j in range(SLOT_TILES - 3, SLOT_TILES):
                    y_out(j, j)

            def attention():
                act.wait_ge(weights_ps, 1)
                nc.scalar.activation(w_qkv[:, :], bank[7][:, 0:3 * P], ACT.Copy)
                nc.scalar.activation(w_out[:, :], bank[7][:, 3 * P:4 * P], ACT.Copy).then_inc(weights_sb, 1)
                transposed(1)
                for i in range(8):
                    act.wait_ge(qk_ps, i + 1)
                    at_least(act, parts_stored[i % 2], 16 * (i // 2))
                    nc.scalar.activation(part_sb[i % 2][:, 0, :], bank[4 + i % 2][:, :], ACT.Copy).then_inc(part0_sb, 1)
                    act.wait_ge(rest_ready, i + 1)
                    nc.scalar.activation(part_sb[i % 2][:, 1, :], rest_sb[i % 2], ACT.Copy).then_inc(part1_sb, 1)

                def m_out(u):
                    act.wait_ge(mT_ps, u + 1)
                    if not (isinstance(u, int) and u == 0):
                        act.wait_ge(score_ps, STEPS * (u - 1) + 1)
                    nc.scalar.activation(mT[:, :], bank[7][0:3 * MBLOCKS, 0:P // 2].bitcast(BF16), ACT.Copy).then_inc(mT_ready, 1)

                def unit(u, s):
                    for c in range(CHUNKS):
                        for h in range(GH):
                            i = c * GH + h
                            act.wait_ge(score_ps, STEPS * u + i + 1)
                            at_least(act, pv_done, CHUNKS * u + c - 1)
                            nc.scalar.activation(prob[i % 8], bank[4 + i % 2][:, :], ACT.Exp, scale=SCALE).then_inc(prob_ready, 1)
                            if i == 6 and not (isinstance(u, int) and u == 0):
                                sums_out(u - 1)
                            if i == 26 and not (isinstance(u, int) and u == UNITS - 1):
                                m_out(u + 1)

                def sums_out(u):
                    act.wait_ge(pv_done, CHUNKS * (u + 1))
                    at_least(act, o_ps, u)
                    nc.scalar.activation(oT[:, :], bank[6], ACT.Copy).then_inc(oT_ready, 1)

                m_out(0)
                for i in range(2):
                    act.wait_ge(parts_stored[i], 64)
                for s in range(4):
                    unit(s, s)
                with act.Fori(1, GROUPS // 2 - 1) as k:
                    for s in range(4):
                        unit(4 * k + s, s)
                for s in range(4):
                    unit(UNITS - 4 + s, s)
                sums_out(UNITS - 1)

                for g in range(QUADS):
                    act.wait_ge(yT_ps, g + 1)
                    nc.scalar.activation(xnT[:, g * BANK:(g + 1) * BANK], bank[g % 2], ACT.Copy).then_inc(yT_ready, 1)

            ffn(0)
            attention()
            ffn(1)

        @block.vector
        def _(dve):
            own = Tally(dve_own)

            def after(ins):
                dve.wait_ge(dve_own, own.done(ins))

            def normalize(use):
                def statistics(g):
                    if use == 0:
                        dve.wait_ge(x_loaded[g], 16)
                    elif use == 2:
                        dve.wait_ge(proj_ps, g + 1)
                        after(nc.vector.tensor_tensor(xres[:, quad(g), :], xres[:, quad(g), :],
                                                      bank[4 + g % 2].rearrange("p (t h) -> p t h", h=P), ALU.add))
                    else:
                        dve.wait_ge(y_loaded[g], 16 * ((use + 1) // 2))
                        ins = nc.vector.scalar_tensor_tensor(out=xres[:, quad(g), :], in0=y_back[:, quad(g), :], scalar=0.5,
                                                             in1=xres[:, quad(g), :], op0=ALU.mult, op1=ALU.add)
                        if use == 3:
                            ins.then_inc(xn_ready, 1)
                            return
                        after(ins)
                    for t in range(4 * g, 4 * g + 4):
                        ins = nc.vector.bn_stats(stats[:, t, :], xres[:, t, :])
                    after(ins)
                    for t in range(4 * g, 4 * g + 4):
                        ins = nc.vector.bn_aggr(mv[:, t, :], stats[:, t, :])
                    after(ins)
                    nc.vector.tensor_scalar(var[:, quad(g)], mv[:, quad(g), 1], EPS, None, ALU.add).then_inc(var_ready, 1)

                def rows(g):
                    r = rstd[:, quad(g)]
                    dve.wait_ge(std_ready, use * QUADS + g + 1)
                    after(nc.vector.reciprocal(r, std[:, quad(g)]))
                    after(nc.vector.tensor_tensor(newton[:, :], r, r, ALU.mult))
                    after(nc.vector.tensor_tensor(newton[:, :], newton[:, :], var[:, quad(g)], ALU.mult))
                    after(nc.vector.tensor_scalar(newton[:, :], newton[:, :], -0.5, 1.5, ALU.mult, ALU.add))
                    after(nc.vector.tensor_tensor(r, r, newton[:, :], ALU.mult))
                    if use == 2:
                        dve.wait_ge(yT_ps, QUADS)
                    for t in range(4 * g, 4 * g + 4):
                        ins = nc.vector.tensor_scalar(xn_tile(t), xres[:, t, :], mv[:, t, 0:1], rstd[:, t:t + 1],
                                                      ALU.subtract, ALU.mult)
                    ins.then_inc(xn_ready, 1)

                for g in range(QUADS + 1):
                    if g < QUADS:
                        statistics(g)
                    if g and use != 3:
                        rows(g - 1)

            def ffn(n):
                dve.wait_ge(consts_ready, 2)
                normalize(2 * n)
                logits = bank[2].rearrange("p (t e) -> p t e", e=EXPERTS)
                wide = lambda a: a.unsqueeze(2).broadcast_to([P, TILES, EXPERTS])
                rev3 = rev[:, :].unsqueeze(1).broadcast_to([P, TILES, EXPERTS])
                dve.wait_ge(logits_ready, n + 1)
                ins = nc.vector.tensor_reduce(top[:, :], logits, AX_X, ALU.max)
                ins.then_inc(top_ready, 1)
                dve.wait_ge(top_ready, n + 1)
                after(nc.vector.tensor_tensor(hit, logits, wide(top[:, :]), ALU.is_equal))
                after(nc.vector.tensor_tensor(cand, hit, rev3, ALU.mult))
                after(nc.vector.tensor_reduce(rtop[:, :], cand, AX_X, ALU.max))
                nc.vector.tensor_tensor(onehot3, rev3, wide(rtop[:, :]), ALU.is_equal).then_inc(onehot_ready, 1)

                def sh_product(i):
                    dve.wait_ge(shsilu_sb, 8 * n + i + 1)
                    at_least(dve, shy_ps, 4 * n + i // 2 - 1)
                    nc.vector.tensor_tensor(h_sh[i // 2 % 2][i % 2], bank[1 + 5 * (i % 2)][:, :], silu_sb[i % 2],
                                            ALU.mult).then_inc(shh_sb, 1)

                def sh_add(q):
                    dve.wait_ge(shy_ps, 4 * n + q + 1)
                    nc.vector.scalar_tensor_tensor(out=xres[:, quad(q), :], in0=bank[7].rearrange("p (t h) -> p t h", h=P),
                                                   scalar=0.5, in1=xres[:, quad(q), :], op0=ALU.mult, op1=ALU.add)\
                        .then_inc(shy_added, 1)

                dve.wait_ge(escore_ready, n + 1)
                after(nc.vector.tensor_scalar(escore[:, :], escore[:, :], 1.0, None, ALU.add))
                after(nc.vector.reciprocal(score[:, :], escore[:, :]))
                sh_product(0)
                sh_product(1)
                after(nc.vector.tensor_tensor(xn[:, :, 0:P], xn[:, :, 0:P], score[:, :].unsqueeze(2).broadcast_to([P, TILES, P]), ALU.mult))
                dve.wait_ge(ranks_ready, n + 1)
                count = bank[4][:, 0:EXPERTS]
                after(nc.vector.tensor_scalar(count_i[:, :], count, float(P - 1), None, ALU.add))
                after(nc.vector.tensor_scalar(count_i[:, :], count_i[:, :], 7, 7, ALU.logical_shift_right, ALU.logical_shift_left))
                after(nc.vector.tensor_copy(slots_of[:, :], count_i[:, :]))
                after(nc.vector.tensor_tensor_scan(slots_to[:, :], slots_of[:, :], zeros[:, :], 0.0, ALU.add, ALU.add))
                after(nc.vector.tensor_tensor(base_e[:, :], slots_to[:, :], slots_of[:, :], ALU.subtract))
                after(nc.vector.tensor_tensor(place, bank[3].rearrange("p (t e) -> p t e", e=EXPERTS),
                                              base_e[:, :].unsqueeze(1).broadcast_to([P, TILES, EXPERTS]), ALU.add))
                after(nc.vector.tensor_tensor(place, place, onehot3, ALU.mult))
                after(nc.vector.tensor_reduce(slot_f[:, :], place, AX_X, ALU.add))
                nc.vector.tensor_copy(slot_i[:, :], slot_f[:, :]).then_inc(slots_ready, 1)
                after(nc.vector.tensor_scalar(below[:, :], slots_to[:, :], 1.0 / P, None, ALU.mult))
                after(nc.vector.tensor_scalar(below[:, :], below[:, :], slot_tile[:, 0:1], None, ALU.is_le))
                after(nc.vector.tensor_reduce(eid[:, :], below[:, :], AX_X, ALU.add))
                nc.vector.tensor_scalar(eid[:, :], eid[:, :], float(EXPERTS - 1), float(WROW), ALU.min, ALU.mult).then_inc(eid_ready, 1)
                sh_product(2)
                sh_product(3)
                sh_add(0)
                dve.wait_ge(eid_row, n + 1)
                nc.vector.tensor_copy(woff[:, :], bank[4][0:1, P:2 * P]).then_inc(woff_ready, 1)
                sh_product(4)
                sh_product(5)
                sh_add(1)
                sh_product(6)
                sh_product(7)
                sh_add(2)
                sh_add(3)

                base = n * SLOT_TILES

                def hT_out(j, r):
                    dve.wait_ge(hT_ps, base + j + 1)
                    at_least(dve, y_ps, base + j - 1)
                    nc.vector.tensor_copy(hT_sb[r % 2], bank[2 + r % 2][:, 0:INNER]).then_inc(hT_done, 1)

                def product(j, r):
                    dve.wait_ge(silu_done, base + j + 1)
                    at_least(dve, hT_ps, base + j - 1)
                    nc.vector.tensor_tensor(h_sb[r % 2], bank[r % 2][:, INNER:2 * INNER], silu_sb[r % 2][:, 0:INNER],
                                            ALU.mult).then_inc(h_done, 1)

                def ids(j, r):
                    dve.wait_ge(xe_loaded[r % 4], 4 * (base + j - r % 4) + 16)
                    at_least(dve, y_stored[r % 4], 4 * (base + j - r % 4) - 16)
                    nc.vector.tensor_copy(slot_token[:, r % 8:r % 8 + 1], xe[r % 4][:, P:P + 1].bitcast(I32)).then_inc(ids_done, 1)

                def turn(j, r):
                    product(j, r)
                    if not isinstance(j, int) or j >= 2:
                        hT_out(j - 2, r)
                    if not isinstance(j, int) or j + 1 < SLOT_TILES:
                        ids(j + 1, r + 1)

                ids(0, 0)
                for j in range(8):
                    turn(j, j)
                with dve.Fori(1, SLOT_TILES // 8 - 1) as k:
                    for r in range(8):
                        turn(8 * k + r, r)
                for j in range(SLOT_TILES - 8, SLOT_TILES):
                    turn(j, j)
                for j in range(SLOT_TILES - 2, SLOT_TILES):
                    hT_out(j, j)

            def attention():
                normalize(1)
                def split(i):
                    dve.wait_ge(part0_sb, i + 1)
                    nc.vector.tensor_tensor(rest_sb[i % 2], bank[4 + i % 2][:, :], part_sb[i % 2][:, 0, :],
                                            ALU.subtract).then_inc(rest_ready, 1)
                    dve.wait_ge(part1_sb, i + 1)
                    dve.wait_ge(rest_ready, i + 1)
                    nc.vector.tensor_tensor(part_sb[i % 2][:, 2, :], rest_sb[i % 2], part_sb[i % 2][:, 1, :],
                                            ALU.subtract).then_inc(part2_sb, 1)

                def values_out(i):
                    dve.wait_ge(v_ps, i + 1)
                    b, c0 = i // 2, 4 * (i % 2)
                    src = bank[6 + i % 2][:, :].rearrange("p (c g h d) -> p g c h d", c=4, g=HEADS // GH, h=GH)
                    for g in range(HEADS // GH):
                        ins = nc.vector.tensor_copy(v_all5[:, b * GH + g, c0:c0 + 4, :, 0:HD], src[:, g])
                    ins.then_inc(v_sb, 1)

                dve.wait_ge(stacks_cleared, 1)
                for b in range(2):
                    for i in range(4 * b, 4 * b + 4):
                        split(i)
                    values_out(2 * b)
                    values_out(2 * b + 1)

                def row_max(u, m):
                    i = MBLOCKS * u[0] + m
                    dve.wait_ge(smax_ps, i + 1)
                    at_least(dve, mparts_ready, u[0] - 1)
                    nc.vector.tensor_reduce(rowmax[u[1] % 2][:, m:m + 1], pair[m % 2][:, :], AX_X, ALU.max).then_inc(smax_read, 1)

                def store_norm(u, b, g, half):
                    dve.wait_ge(o_ps, u + 1)
                    o = bank[7].rearrange("p (t h d) -> p t h d", t=4, h=GH)
                    after(nc.vector.reciprocal(rden[:, :, :], o[:, :, :, HD]))
                    t0 = 8 * b + 4 * half
                    for t in range(4):
                        dst = xn[:, bass.ds(t0 + t, 1), bass.ds(g * GH * HD, GH * HD)].rearrange("p o (h d) -> p (o h) d", d=HD)
                        ins = nc.vector.tensor_tensor(dst, o[:, t, :, 0:HD],
                                                      rden[:, t, :].unsqueeze(2).broadcast_to([P, GH, HD]), ALU.mult)
                    ins.then_inc(o_normed, 1)

                def unit(u, s, b, g, first=False, last=9):
                    order = [((u + 1, s + 1), m) for m in range(AHEAD, MBLOCKS)] + [((u + 2, s + 2), m) for m in range(AHEAD)]
                    for i, (v, m) in enumerate(order):
                        if v[1] - s < last:
                            row_max(v, m)
                        if i == 5 and not first:
                            store_norm(u - 1, b, g, (s + 1) % 2)

                for m in range(MBLOCKS):
                    row_max((0, 0), m)
                for m in range(AHEAD):
                    row_max((1, 1), m)
                unit(0, 0, 0, 0, first=True)
                for s in range(1, 4):
                    unit(s, s, 0, (s - 1) // 2)
                start = own.n
                per = 4
                with dve.Fori(1, GROUPS // 2 - 1) as k:
                    own.base, own.n = start + (k - 1) * per, 0
                    unit(4 * k, 0, 0, 2 * k - 1)
                    for s in range(1, 4):
                        unit(4 * k + s, s, k - 1, 4 - 2 * k + (s - 1) // 2)
                    assert own.n == per
                own.base, own.n = 0, start + per * (GROUPS // 2 - 2)
                unit(UNITS - 4, 0, 1, 1)
                unit(UNITS - 3, 1, 1, 2)
                unit(UNITS - 2, 2, 1, 2, last=2)
                unit(UNITS - 1, 3, 1, 3, last=1)
                store_norm(UNITS - 1, 1, 3, 1)

            ffn(0)
            attention()
            ffn(1)
            normalize(3)

        @block.tensor
        def _(pe):
            pe.wait_ge(consts_ready, 2)

            def transposes(use):
                for g in range(QUADS):
                    pe.wait_ge(xn_ready, use * QUADS + g + 1)
                    at_least(pe, xnT_ready, use * QUADS + g - 1)
                    for t in range(4):
                        ins = nc.tensor.transpose(bank[g % 2][:, t * P:(t + 1) * P], xn_tile(4 * g + t), identf[:, :])
                    ins.then_inc(xnT_ps, 1)

            def ffn(n):
                transposes(2 * n)
                if n == 0:
                    pe.wait_ge(small_loaded, 16 * 8)
                for t in range(TILES):
                    pe.wait_ge(xnT_ready, (2 * n) * QUADS + t // 4 + 1)
                    ins = nc.tensor.matmul(bank[2][:, t * EXPERTS:(t + 1) * EXPERTS], xnT[:, t * P:(t + 1) * P], gate_sb[:, :],
                                           start=True, stop=True)
                ins.then_inc(logits_ready, 1)

                def sh_up(q):
                    for c in range(2):
                        i = 2 * q + c
                        at_least(pe, shh_sb, 8 * n + i - 1)
                        for part, b in ((0, bank[5 * c]), (INNER, bank[1 + 5 * c])):
                            ins = nc.tensor.matmul(b[:, :], w_sh[:, part + c * P:part + (c + 1) * P], xnT[:, q * BANK:(q + 1) * BANK],
                                                   start=True, stop=True)
                        ins.then_inc(shg_ps, 1)

                def sh_down(q):
                    pe.wait_ge(shh_sb, 8 * n + 2 * q + 2)
                    at_least(pe, shy_added, 4 * n + q)
                    for t in range(4):
                        for c in range(2):
                            ins = nc.tensor.matmul(bank[7][:, t * P:(t + 1) * P], h_sh[q % 2][c][:, t * P:(t + 1) * P],
                                                   w_sh[:, 2 * INNER + c * P:2 * INNER + (c + 1) * P], start=(c == 0), stop=(c == 1))
                    ins.then_inc(shy_ps, 1)

                sh_up(0)
                pe.wait_ge(onehot_ready, n + 1)
                for t in range(TILES):
                    nc.tensor.matmul(bank[4][:, 0:EXPERTS], onesb[:, :], onehot[:, t * EXPERTS:(t + 1) * EXPERTS],
                                     start=(t == 0), stop=(t == TILES - 1))
                nc.tensor.matmul(bank[3], before[:, :], onehot, start=True, stop=False)
                for d in range(1, TILES):
                    ins = nc.tensor.matmul(bank[3][:, d * EXPERTS:], onesb[:, :], onehot[:, 0:(TILES - d) * EXPERTS],
                                           start=False, stop=(d == TILES - 1))
                ins.then_inc(ranks_ready, 1)
                sh_up(1)
                sh_down(0)
                pe.wait_ge(eid_ready, n + 1)
                nc.tensor.matmul(bank[4][0:1, P:2 * P], eid[:, :], identf[:, :], start=True, stop=True).then_inc(eid_row, 1)
                sh_up(2)
                sh_down(1)
                sh_up(3)
                sh_down(2)
                sh_down(3)

                base = n * SLOT_TILES

                def x_transpose(j, r):
                    pe.wait_ge(xe_loaded[r % 4], 4 * (base + j - r % 4) + 16)
                    at_least(pe, xeT_sb, base + j - 1)
                    nc.tensor.transpose(bank[5 + r % 2][:, 0:P], xe[r % 4][:, 0:P], identf[:, :]).then_inc(xeT_ps, 1)

                def gate_up(j, r):
                    e = pe.value_load(woff[0:1, bass.ds(j, 1)], min_val=0, max_val=(EXPERTS - 1) * WROW)
                    pe.wait_ge(xeT_sb, base + j + 1)
                    at_least(pe, h_done, base + j - 1)
                    nc.tensor.matmul(bank[r % 2][:, :], xeT[r % 2][:, :], w_exp[:, bass.ds(e, 2 * INNER)],
                                     start=True, stop=True).then_inc(gu_ps, 1)

                def h_transpose(j, r):
                    pe.wait_ge(h_done, base + j + 1)
                    at_least(pe, hT_done, base + j - 1)
                    for c in range(2):
                        ins = nc.tensor.transpose(bank[2 + r % 2][:, c * P:(c + 1) * P], h_sb[r % 2][:, c * P:(c + 1) * P], identf[:, :])
                    ins.then_inc(hT_ps, 1)

                def down(j, r):
                    e = pe.value_load(woff[0:1, bass.ds(j, 1)], min_val=0, max_val=(EXPERTS - 1) * WROW)
                    pe.wait_ge(hT_done, base + j + 1)
                    at_least(pe, y_done, base + j - 1)
                    for c in range(2):
                        ins = nc.tensor.matmul(bank[(4, 7)[r % 2]][:, 0:P], hT_sb[r % 2][:, c * P:(c + 1) * P],
                                               w_exp[:, bass.ds(e + 2 * INNER + c * P, P)], start=(c == 0), stop=(c == 1))
                    ins.then_inc(y_ps, 1)

                pe.wait_ge(woff_ready, n + 1)
                pe.wait_ge(experts_loaded, 16 * 16)
                pe.wait_ge(shy_added, 4 * (n + 1))

                def turn(j, r):
                    if not isinstance(j, int) or j + 1 < SLOT_TILES:
                        x_transpose(j + 1, r + 1)
                    gate_up(j, r)
                    if not isinstance(j, int) or j >= 2:
                        h_transpose(j - 2, r)
                    if not isinstance(j, int) or j >= 3:
                        down(j - 3, r + 1)

                x_transpose(0, 0)
                for j in range(8):
                    turn(j, j)
                with pe.Fori(1, SLOT_TILES // 8 - 1) as k:
                    for r in range(8):
                        turn(8 * k + r, r)
                for j in range(SLOT_TILES - 8, SLOT_TILES):
                    turn(j, j)
                h_transpose(SLOT_TILES - 2, 0)
                down(SLOT_TILES - 3, 1)
                h_transpose(SLOT_TILES - 1, 1)
                down(SLOT_TILES - 2, 0)
                down(SLOT_TILES - 1, 1)

            def attention():
                pe.wait_ge(y_done, SLOT_TILES)
                nc.tensor.matmul(bank[7][:, 0:3 * P], wv_sb[:, :], wut_sb[:, :], start=True, stop=True)
                nc.tensor.matmul(bank[7][:, 3 * P:4 * P], wov_sb[:, :], wout_sb[:, :], start=True, stop=True).then_inc(weights_ps, 1)
                transposes(1)
                pe.wait_ge(weights_sb, 1)
                for b in range(2):
                    for i in range(4 * b, 4 * b + 4):
                        qk, half = i // 2 % 2, i % 2
                        pe.wait_ge(xnT_ready, QUADS + 2 * b + half + 1)
                        at_least(pe, rest_ready, i - 1)
                        nc.tensor.matmul(bank[4 + i % 2][:, :], w_qkv[:, qk * P:(qk + 1) * P],
                                         xnT[:, (2 * b + half) * BANK:(2 * b + half + 1) * BANK], start=True, stop=True).then_inc(qk_ps, 1)
                    for i in range(2 * b, 2 * b + 2):
                        at_least(pe, v_sb, i - 1)
                        for c in range(4):
                            t = 4 * i + c
                            ins = nc.tensor.matmul(bank[6 + i % 2][:, c * P:(c + 1) * P], xnT[:, t * P:(t + 1) * P],
                                                   w_qkv[:, 2 * P:3 * P], start=True, stop=True)
                        ins.then_inc(v_ps, 1)
                pe.wait_ge(v_sb, 4)
                pe.wait_ge(rest_ready, 8)

                def max_scores(u, m, part):
                    h, t, i = m // 4, m % 4, MBLOCKS * u[0] + m
                    r, half = u[1] // 2 % 2, u[1] % 2
                    if part == 0:
                        at_least(pe, smax_read, i - 1)
                    ins = nc.tensor.matmul(pair[m % 2][:, part * BANK:(part + 1) * BANK], q_stack[r][0:MROW, half, h, t * P:(t + 1) * P],
                                           k_stack[r][0:MROW, h, part * BANK:(part + 1) * BANK], start=True, stop=True)
                    if part == 1:
                        ins.then_inc(smax_ps, 1)

                def scores(u, s, i):
                    c, h, r, half = i // GH, i % GH, s // 2 % 2, s % 2
                    at_least(pe, prob_ready, STEPS * u + i - 1)
                    nc.tensor.matmul(bank[4 + i % 2][:, :], k_stack[r][:, h, c * P:(c + 1) * P],
                                     q_stack[r][:, half, h, :], start=True, stop=True).then_inc(score_ps, 1)

                def weigh(u, s, c):
                    pe.wait_ge(prob_ready, STEPS * u + GH * (c + 1))
                    if c == 0:
                        at_least(pe, oT_ready, u)
                    for h in range(GH):
                        ins = nc.tensor.matmul(bank[6][32 * h:32 * (h + 1), :], v_grp[s // 2 % 2][:, c, h, :], prob[(c * GH + h) % 8],
                                               start=(c == 0), stop=(c == CHUNKS - 1))
                    ins.then_inc(pv_done, 1)

                def o_transpose(u):
                    pe.wait_ge(oT_ready, u + 1)
                    at_least(pe, o_normed, u)
                    at_least(pe, mT_ready, u + 2 if not isinstance(u, int) or u + 2 <= UNITS else UNITS)
                    for t in range(4):
                        ins = nc.tensor.transpose(bank[7][:, t * P:(t + 1) * P], oT[:, t * P:(t + 1) * P], identf[:, :])
                    ins.then_inc(o_ps, 1)

                def m_transpose(u):
                    pe.wait_ge(mparts_ready, u + 1)
                    at_least(pe, o_normed, u - 1)
                    nc.tensor.transpose(bank[7][:, 0:P // 2].bitcast(BF16),
                                        mpart[:, :, :].rearrange("p c m -> p (c m)"), identb[:, :]).then_inc(mT_ps, 1)

                def unit(u, s, quarter, first=False, last=9):
                    if s % 2 == 0:
                        pe.wait_ge(vgrp_ready, 2 * quarter + s // 2 + 1)
                    pe.wait_ge(m_loaded[s % 2], 48 * (2 * quarter + s // 2 + 1))
                    order = [((u + 1, s + 1), m) for m in range(AHEAD, MBLOCKS)] + [((u + 2, s + 2), m) for m in range(AHEAD)]
                    for i in range(STEPS):
                        scores(u, s, i)
                        v, m = order[i // 2]
                        if v[1] - s < last:
                            if i == 2 * (MBLOCKS - AHEAD) and s % 2 == 0:
                                pe.wait_ge(stack_loaded[(s // 2 + 1) % 2], 16 * 18 * (quarter + (s + 2) // 4 + 1))
                            max_scores(v, m, i % 2)
                        if i % GH == GH - 1 and i >= GH:
                            weigh(u, s, i // GH - 1)
                        if i == GH - 1 and not first:
                            weigh(u - 1, s - 1 + 4, CHUNKS - 1)
                        if i == 10 and not first:
                            o_transpose(u - 1)
                        if i == 25 and last > 1:
                            m_transpose(u + 1)

                pe.wait_ge(stack_loaded[0], 16 * 18)
                for m in range(MBLOCKS):
                    for part in range(2):
                        max_scores((0, 0), m, part)
                for m in range(AHEAD):
                    for part in range(2):
                        max_scores((1, 1), m, part)
                    if m == 2:
                        m_transpose(0)
                for s in range(4):
                    unit(s, s, 0, first=(s == 0))
                with pe.Fori(1, GROUPS // 2 - 1) as k:
                    for s in range(4):
                        unit(4 * k + s, s, k)
                for s in range(4):
                    unit(UNITS - 4 + s, s, GROUPS // 2 - 1, last=(9, 9, 2, 1)[s])
                weigh(UNITS - 1, 3, CHUNKS - 1)
                o_transpose(UNITS - 1)

                pe.wait_ge(o_normed, UNITS)
                for g in range(QUADS + 1):
                    if g < QUADS:
                        at_least(pe, yT_ready, g - 1)
                        for t in range(4):
                            ins = nc.tensor.transpose(bank[g % 2][:, t * P:(t + 1) * P], xn_tile(4 * g + t), identf[:, :])
                        ins.then_inc(yT_ps, 1)
                    if g:
                        pe.wait_ge(yT_ready, g)
                        if g > 2:
                            pe.wait_ge(xn_ready, 2 * QUADS + g - 2)
                        for t in range(4):
                            at = ((g - 1) * 4 + t) * P
                            ins = nc.tensor.matmul(bank[4 + (g - 1) % 2][:, t * P:(t + 1) * P], xnT[:, at:at + P], w_out[:, :],
                                                   start=True, stop=True)
                        ins.then_inc(proj_ps, 1)

            ffn(0)
            attention()
            ffn(1)


_ORDER = ["x", "w_qkv_v", "w_qkv_ut", "w_o_v", "w_o_ut", "gate_w", "sh_gate", "sh_up", "sh_down", "r_gate", "r_up", "r_down"]


def kernel(L0_attn_x, L0_attn_W_qkv_v, L0_attn_W_qkv_u, L0_attn_W_o_v, L0_attn_W_o_u, L0_ffn_gate_w,
           L0_ffn_shared_gate_w, L0_ffn_shared_up_w, L0_ffn_shared_down_w, L0_ffn_routed_gate_w,
           L0_ffn_routed_up_w, L0_ffn_routed_down_w):
    import numpy as np
    import concourse.bacc as bacc
    from concourse.bass_utils import run_bass_kernel_spmd

    arrays = [L0_attn_x, L0_attn_W_qkv_v, np.asarray(L0_attn_W_qkv_u).T, L0_attn_W_o_v, np.asarray(L0_attn_W_o_u).T,
              L0_ffn_gate_w, L0_ffn_shared_gate_w, L0_ffn_shared_up_w, L0_ffn_shared_down_w, L0_ffn_routed_gate_w,
              L0_ffn_routed_up_w, L0_ffn_routed_down_w]
    nc = bacc.Bacc("TRN2", target_bir_lowering=False, num_devices=1)
    given, args = {}, []
    for name, a in zip(_ORDER, arrays):
        a = np.ascontiguousarray(a)
        given[f"in_{name}"] = a
        args.append(nc.dram_tensor(f"in_{name}", a.shape, mybir.dt.from_np(a.dtype), kind="ExternalInput").ap())
    out = nc.dram_tensor("out", given["in_x"].shape, F32, kind="ExternalOutput").ap()
    build(nc, *args, out)
    return run_bass_kernel_spmd(nc, [given], core_ids=[0]).results[0]["out"]
```

```python
from contextlib import ExitStack

import concourse.bass as bass
from concourse import mybir

F32 = mybir.dt.float32
BF16 = mybir.dt.bfloat16
I32 = mybir.dt.int32
U32 = mybir.dt.uint32
ALU = mybir.AluOpType
ACT = mybir.ActivationFunctionType
AX_X = mybir.AxisListType.X

P = 128
BANK = 512
TILES = 16
QUADS = TILES // 4
TOKENS = TILES * P
EXPERTS = 32
INNER = 256
WROW = 3 * INNER
SLOT_TILES = 48
ROW = P + 4
NOWHERE = 4 * TOKENS
EPS = 1e-5

HEADS = 16
HD = 8
SEQ = 1024
GH = 4
GROUPS = 2 * HEADS // GH
UNITS = 2 * GROUPS
CHUNKS = SEQ // P
QW = 512
STEPS = CHUNKS * GH
AHEAD = 6
MBLOCKS = GH * QW // P
Q_OF_K = (3, 2, 1)
MROW = 96
SCALE = float(HD) ** -0.5


class Tally:

    def __init__(self, sem):
        self.sem, self.base, self.n = sem, 0, 0

    def done(self, ins):
        ins.then_inc(self.sem, 1)
        self.n += 1
        return self.base + self.n


ORDER = [(1, m) for m in range(AHEAD, MBLOCKS)] + [(2, m) for m in range(AHEAD)]
MAXIMA = [ORDER[2 * c:2 * c + 2] for c in range(CHUNKS)]


def at_least(eng, sem, value):
    if not isinstance(value, int) or value > 0:
        eng.wait_ge(sem, value)


def build(nc, x_in, w_qkv_v, w_qkv_ut, w_o_v, w_o_ut, gate_w, sh_gate, sh_up, sh_down, r_gate, r_up, r_down, out):
    x_view = x_in.rearrange("b (t p) h -> p (b t) h", p=P)
    out_view = out.rearrange("b (t p) h -> p (b t) h", p=P)

    with ExitStack() as ctx:
        def sb(name, shape, dt=F32):
            return ctx.enter_context(nc.sbuf_tensor(name, shape, dt))

        def sem(name):
            return ctx.enter_context(nc.semaphore(name))

        rows_dram = [nc.dram_tensor(f"rows{n}", (SLOT_TILES * P, ROW), F32, kind="Internal").ap() for n in range(2)]
        y_dram = [nc.dram_tensor(f"y{n}", (TOKENS, P), F32, kind="Internal").ap() for n in range(2)]
        q_dram = nc.dram_tensor("q_parts", (3, 2 * P // GH, GH * SEQ), BF16, kind="Internal").ap()
        k_dram = nc.dram_tensor("k_parts", (3, 2 * P, SEQ), BF16, kind="Internal").ap()

        pair = [ctx.enter_context(nc.psum_tensor(f"pair{i}", [P, 2 * BANK], F32)) for i in range(2)]
        bank = [pair[i // 2][:, i % 2 * BANK:(i % 2 + 1) * BANK] for i in range(4)]
        bank += [ctx.enter_context(nc.psum_tensor(f"bank{i}", [P, BANK], F32))[:, :] for i in range(4, 8)]

        w_exp = sb("w_exp", [P, EXPERTS * WROW])
        w_sh = sb("w_sh", [P, WROW])
        gate_sb = sb("gate_sb", [P, EXPERTS])
        wv_sb = sb("wv_sb", [32, P])
        wut_sb = sb("wut_sb", [32, 3 * P])
        wov_sb = sb("wov_sb", [32, P])
        wout_sb = sb("wout_sb", [32, P])
        w_qkv = sb("w_qkv", [P, 3 * P])
        w_out = sb("w_out", [P, P])

        xres = sb("xres", [P, TILES, P])
        xn = sb("xn", [P, TILES, ROW])
        xnT = sb("xnT", [P, TOKENS])
        y_back = xnT[:, :].rearrange("p (t h) -> p t h", h=P)

        identf = sb("identf", [P, P])
        identb = sb("identb", [P, P], BF16)
        before = sb("before", [P, P], BF16)
        onesb = sb("onesb", [P, P], BF16)
        iota_i = sb("iota_i", [P, EXPERTS], I32)
        rev = sb("rev", [P, EXPERTS])
        slot_tile_i = sb("slot_tile_i", [P, 1], I32)
        slot_tile = sb("slot_tile", [P, 1])
        zeros = sb("zeros", [P, EXPERTS])
        empty_row = sb("empty_row", [P, ROW])

        stats = sb("stats", [P, TILES, 6])
        mv = sb("mv", [P, TILES, 2])
        var = sb("var", [P, TILES])
        std = sb("std", [P, TILES])
        rstd = sb("rstd", [P, TILES])
        newton = sb("newton", [P, TILES])
        shift = sb("shift", [P, TILES])
        top = sb("top", [P, TILES])
        rtop = sb("rtop", [P, TILES])
        escore = sb("escore", [P, TILES])
        score = sb("score", [P, TILES])
        count_i = sb("count_i", [P, EXPERTS], I32)
        slots_of = sb("slots_of", [P, EXPERTS])
        slots_to = sb("slots_to", [P, EXPERTS])
        base_e = sb("base_e", [P, EXPERTS])
        below = sb("below", [P, EXPERTS])
        eid = sb("eid", [P, 1])
        slot_f = sb("slot_f", [P, TILES])
        slot_i = sb("slot_i", [P, TILES], I32)
        woff = sb("woff", [1, P], I32)

        xe = [sb(f"xe{i}", [P, ROW]) for i in range(4)]
        xeT = [sb(f"xeT{i}", [P, P]) for i in range(2)]
        yb = [sb(f"yb{i}", [P, P]) for i in range(4)]
        slot_token = sb("slot_token", [P, 8], I32)

        arena = sb("arena", [P, 8 * BANK])
        silu_sb = [arena[:, i * BANK:(i + 1) * BANK] for i in range(2)]
        h_sh = [[arena[:, (2 + 2 * i + c) * BANK:(3 + 2 * i + c) * BANK] for c in range(2)] for i in range(2)]
        h_sb = [arena[:, 6 * BANK + i * INNER:6 * BANK + (i + 1) * INNER] for i in range(2)]
        hT_sb = [arena[:, 7 * BANK + i * INNER:7 * BANK + (i + 1) * INNER] for i in range(2)]
        part_sb = [arena[:, i * 768:(i + 1) * 768].bitcast(BF16).rearrange("p (c t) -> p c t", c=3) for i in range(4)]
        rest_sb = [arena[:, (6 + i) * BANK:(7 + i) * BANK] for i in range(2)]
        prob = [arena[:, i * BANK:(i + 1) * BANK] for i in range(8)]

        arena2 = sb("arena2", [P, 2, CHUNKS, GH, 32])
        flat2 = arena2[:, :, :, :, :].rearrange("p a c h d -> p (a c h d)")
        hit = flat2[:, 0:512].rearrange("p (t e) -> p t e", e=EXPERTS)
        cand = flat2[:, 512:1024].rearrange("p (t e) -> p t e", e=EXPERTS)
        place = flat2[:, 1024:1536].rearrange("p (t e) -> p t e", e=EXPERTS)
        onehot = flat2[:, 1536:1792].bitcast(BF16)
        onehot3 = onehot.rearrange("p (t e) -> p t e", e=EXPERTS)
        v_grp = [arena2[:, i] for i in range(2)]

        v_all = sb("v_all", [P, GROUPS, CHUNKS * GH * (HD + 1)])
        v_all5 = v_all[:, :, :].rearrange("p g (c h d) -> p g c h d", c=CHUNKS, h=GH)
        q_stack = [sb(f"q_stack{i}", [P, 2, GH, QW], BF16) for i in range(2)]
        k_stack = [sb(f"k_stack{i}", [P, GH, SEQ], BF16) for i in range(2)]
        rowmax = [sb(f"rowmax{i}", [P, MBLOCKS]) for i in range(2)]
        mrest = sb("mrest", [P, MBLOCKS])
        mpart = sb("mpart", [P, P // MBLOCKS, MBLOCKS], BF16)
        mT = sb("mT", [3 * MBLOCKS, P], BF16)
        oT = sb("oT", [P, QW])
        rden = sb("rden", [P, 4, GH])

        x_loaded = [sem(f"x_loaded{g}") for g in range(QUADS)]
        small_loaded = sem("small_loaded")
        experts_loaded = sem("experts_loaded")
        consts_ready = sem("consts_ready")
        stacks_cleared = sem("stacks_cleared")
        prefilled = [sem(f"prefilled{n}") for n in range(2)]
        weights_ps = sem("weights_ps")
        weights_sb = sem("weights_sb")
        dve_own = sem("dve_own")
        pool_own = sem("pool_own")
        var_ready = sem("var_ready")
        std_ready = sem("std_ready")
        rstd_ready = sem("rstd_ready")
        xn_ready = sem("xn_ready")
        xn_act_ready = sem("xn_act_ready")
        out_ready = sem("out_ready")
        xnT_ps = sem("xnT_ps")
        xnT_ready = sem("xnT_ready")
        logits_ready = sem("logits_ready")
        top_ready = sem("top_ready")
        escore_ready = sem("escore_ready")
        onehot_ready = sem("onehot_ready")
        ranks_ready = sem("ranks_ready")
        eid_ready = sem("eid_ready")
        eid_row = sem("eid_row")
        woff_ready = sem("woff_ready")
        slots_ready = sem("slots_ready")
        scattered = sem("scattered")
        shg_ps = sem("shg_ps")
        shsilu_sb = sem("shsilu_sb")
        shh_sb = sem("shh_sb")
        shy_ps = sem("shy_ps")
        shy_added = sem("shy_added")
        xe_loaded = [sem(f"xe_loaded{i}") for i in range(4)]
        xeT_ps = sem("xeT_ps")
        xeT_sb = sem("xeT_sb")
        gu_ps = sem("gu_ps")
        silu_done = sem("silu_done")
        h_done = sem("h_done")
        hT_ps = sem("hT_ps")
        hT_done = sem("hT_done")
        y_ps = sem("y_ps")
        y_done = sem("y_done")
        ids_done = sem("ids_done")
        y_stored = [sem(f"y_stored{i}") for i in range(4)]
        stores_begun = sem("stores_begun")
        y_loaded = [sem(f"y_loaded{g}") for g in range(QUADS)]
        qk_ps = sem("qk_ps")
        part0_sb = sem("part0_sb")
        rest_ready = sem("rest_ready")
        rest_pool_ready = sem("rest_pool_ready")
        part1_sb = sem("part1_sb")
        part2_sb = sem("part2_sb")
        parts_stored = [sem(f"parts_stored{i}") for i in range(4)]
        v_ps = sem("v_ps")
        v_sb = sem("v_sb")
        v_act_sb = sem("v_act_sb")
        stack_loaded = [sem(f"stack_loaded{i}") for i in range(2)]
        vgrp_ready = sem("vgrp_ready")
        smax_ps = sem("smax_ps")
        smax_read = sem("smax_read")
        mparts_ready = sem("mparts_ready")
        mT_ps = sem("mT_ps")
        mT_ready = sem("mT_ready")
        m_loaded = [sem(f"m_loaded{i}") for i in range(2)]
        score_ps = sem("score_ps")
        prob_ready = sem("prob_ready")
        pv_done = sem("pv_done")
        oT_ready = sem("oT_ready")
        o_ps = sem("o_ps")
        o_normed = sem("o_normed")
        yT_ps = sem("yT_ps")
        yT_ready = sem("yT_ready")
        proj_ps = sem("proj_ps")
        proj_added = sem("proj_added")
        stored = sem("stored")

        xn_tile = lambda t: xn[:, t, 0:P]
        quad = lambda g: slice(4 * g, 4 * g + 4)

        part_stores = lambda i: 1 if i // 2 % 2 else 3

        score_bank = lambda i, final: bank[(4, 5, 0, 1)[i % 4] if final else 4 + i % 2]

        v_bank = lambda i: bank[(2, 3, 6, 7)[i]]
        values_src = lambda i: v_bank(i).rearrange("p (c g h d) -> p g c h d", c=4, g=HEADS // GH, h=GH)
        values_dst = lambda i, g: v_all5[:, i // 2 * GH + g, 4 * (i % 2):4 * (i % 2) + 4, :, 0:HD]

        block = ctx.enter_context(nc.Block())

        @block.sync
        def _(sp):
            for g in range(QUADS):
                sp.dma_start(xres[:, quad(g), :], x_view[:, quad(g), :]).then_inc(x_loaded[g], 16)
            for dst, src in ((gate_sb[:, :], gate_w), (w_sh[:, 0:INNER], sh_gate), (w_sh[:, INNER:2 * INNER], sh_up),
                             (w_sh[:, 2 * INNER:].rearrange("p (c h) -> p c h", c=2), sh_down.rearrange("(c p) h -> p c h", p=P)),
                             (wv_sb[:, :], w_qkv_v), (wut_sb[:, :], w_qkv_ut), (wov_sb[:, :], w_o_v), (wout_sb[:, :], w_o_ut)):
                sp.dma_start(dst, src).then_inc(small_loaded, 16)
            sp.wait_ge(consts_ready, 1)

            def prefill(n):
                sp.dma_start(rows_dram[n].rearrange("(j p) r -> p j r", p=P),
                             empty_row[:, :].unsqueeze(1).broadcast_to([P, SLOT_TILES, ROW])).then_inc(prefilled[n], 16)

            prefill(0)
            w3 = w_exp[:, :].rearrange("p (e w) -> p e w", w=WROW)
            step = EXPERTS // 4
            for e in range(0, EXPERTS, step):
                sp.dma_start(w3[:, e:e + step, 0:INNER], r_gate[e:e + step].rearrange("e h i -> h e i")).then_inc(experts_loaded, 16)
                sp.dma_start(w3[:, e:e + step, INNER:2 * INNER], r_up[e:e + step].rearrange("e h i -> h e i")).then_inc(experts_loaded, 16)
                for c in range(2):
                    sp.dma_start(w3[:, e:e + step, 2 * INNER + c * P:2 * INNER + (c + 1) * P],
                                 r_down[e:e + step, c * P:(c + 1) * P, :].rearrange("e p h -> p e h")).then_inc(experts_loaded, 16)
            prefill(1)

            def ffn(n):
                sp.wait_ge(scattered, 16 * TILES * (n + 1))

                def load(j, r):
                    at_least(sp, xeT_ps, n * SLOT_TILES + j - 3)
                    at_least(sp, ids_done, n * SLOT_TILES + j - 3)
                    sp.dma_start(xe[r][:, :], rows_dram[n][bass.ds(j * P, P), :]).then_inc(xe_loaded[r], 16)

                for r in range(4):
                    load(r, r)
                with sp.Fori(1, SLOT_TILES // 4) as k:
                    for r in range(4):
                        load(4 * k + r, r)
                for i in range(4):
                    sp.wait_ge(y_stored[i], 4 * SLOT_TILES * (n + 1))
                y_view = y_dram[n].rearrange("(t p) h -> p t h", p=P)
                for g in range(QUADS):
                    sp.dma_start(y_back[:, quad(g), :], y_view[:, quad(g), :]).then_inc(y_loaded[g], 16)

            def attention():
                def store_parts(i):
                    b, half = i // 4, i % 2
                    sp.wait_ge(part2_sb, i + 1)
                    if i // 2 % 2:
                        sp.dma_start(k_dram[:, b * P:(b + 1) * P, half * QW:(half + 1) * QW].rearrange("c p t -> p c t"),
                                     part_sb[i % 4]).then_inc(parts_stored[i % 4], 16)
                    else:
                        for c in range(3):
                            dst = q_dram[c, b * P // GH:(b + 1) * P // GH, half * GH * QW:(half + 1) * GH * QW]
                            sp.dma_start(dst.rearrange("r (h t) -> r h t", t=QW), part_sb[i % 4][:, c, :])\
                                .then_inc(parts_stored[i % 4], 16)

                def load_stacks(g, r):
                    row = 0
                    for part, n in enumerate(Q_OF_K):
                        rows = slice(row, row + n * HD)
                        row += n * HD
                        q = q_dram[0:n, bass.ds(g * HD, HD), :]
                        k = k_dram[part, bass.ds(g * GH * HD, GH * HD), :].rearrange("(d h) t -> d (h t)", h=GH)
                        sp.dma_start(q_stack[r][rows, :, :, :].rearrange("p a h t -> p (a h t)"), q).then_inc(stack_loaded[r], 16)
                        sp.dma_start(k_stack[r][rows, :, :].rearrange("p h t -> p (h t)"),
                                     k.unsqueeze(0).broadcast_to([n, HD, GH * SEQ])).then_inc(stack_loaded[r], 16)

                def load_m(u):
                    half, r = u[1] % 2, u[1] // 2 % 2
                    sp.wait_ge(mT_ready, u[0] + 1)
                    for c in range(3):
                        dst = q_stack[r][MROW + c:MROW + c + 1, half, :, :].rearrange("o h t -> o (h t)")
                        src = mT[c * MBLOCKS:(c + 1) * MBLOCKS, :]
                        sp.dma_start(dst, src).then_inc(m_loaded[half], 16)

                for i in range(4):
                    store_parts(i)
                sp.wait_ge(stacks_cleared, 1)
                for i in range(4):
                    sp.wait_ge(parts_stored[i], 16 * part_stores(i))
                load_stacks(0, 0)
                load_stacks(1, 1)
                for i in range(4, 8):
                    store_parts(i)
                for i in range(4):
                    sp.wait_ge(parts_stored[i], 32 * part_stores(i))
                load_m((0, 0))
                with sp.Fori(0, GROUPS // 2 - 1) as k:
                    for s in range(4):
                        load_m((4 * k + s + 1, s + 1))
                        if s % 2:
                            sp.wait_ge(pv_done, CHUNKS * (4 * k + s + 1))
                            load_stacks(2 * k + s // 2 + 2, s // 2)
                for s in range(3):
                    load_m((UNITS - 4 + s + 1, s + 1))

            ffn(0)
            attention()
            ffn(1)
            for g in range(QUADS):
                sp.wait_ge(out_ready, g + 1)
                sp.dma_start(out_view[:, quad(g), :], xres[:, quad(g), :]).then_inc(stored, 16)
            sp.wait_ge(stored, 16 * QUADS)

        @block.gpsimd
        def _(pool):
            own = Tally(pool_own)
            nc.gpsimd.memset(empty_row[:, 0:P], 0.0)
            nc.gpsimd.memset(empty_row[:, P:ROW].bitcast(I32), NOWHERE).then_inc(consts_ready, 1)
            nc.gpsimd.memset(identf[:, :], 0.0)
            nc.gpsimd.memset(identb[:, :], 0.0)
            nc.gpsimd.memset(before[:, :], 1.0)
            nc.gpsimd.memset(onesb[:, :], 1.0)
            nc.gpsimd.memset(zeros[:, :], 0.0)
            nc.gpsimd.iota(xn[:, :, P:ROW].bitcast(I32), pattern=[[P, TILES], [0, 4]], base=0, channel_multiplier=1)
            nc.gpsimd.iota(slot_tile_i[:, :], pattern=[[0, 1]], base=0, channel_multiplier=1)
            w = own.done(nc.gpsimd.iota(iota_i[:, :], pattern=[[-1, EXPERTS]], base=EXPERTS, channel_multiplier=0))
            pool.wait_ge(pool_own, w)
            nc.gpsimd.affine_select(out=identf[:, :], in_=identf[:, :], compare_op=ALU.not_equal, fill=1.0,
                                    base=0, pattern=[[-1, P]], channel_multiplier=1)
            nc.gpsimd.affine_select(out=identb[:, :], in_=identb[:, :], compare_op=ALU.not_equal, fill=1.0,
                                    base=0, pattern=[[-1, P]], channel_multiplier=1)
            nc.gpsimd.affine_select(out=before[:, :], in_=before[:, :], compare_op=ALU.is_gt, fill=0.0,
                                    base=0, pattern=[[1, P]], channel_multiplier=-1)
            nc.gpsimd.tensor_copy(slot_tile[:, :], slot_tile_i[:, :])
            nc.gpsimd.tensor_copy(rev[:, :], iota_i[:, :]).then_inc(consts_ready, 1)
            for i in range(2):
                nc.gpsimd.memset(q_stack[i][:, :, :, :].bitcast(F32), 0.0)
                nc.gpsimd.memset(k_stack[i][0:MROW, :, :].bitcast(F32), 0.0)
            pool.wait_ge(pool_own, own.done(nc.gpsimd.memset(v_all[:, :, :], 1.0)))
            for i in range(2):
                w = own.done(nc.gpsimd.memset(k_stack[i][MROW:P, :, :], 1.0))
            pool.wait_ge(pool_own, w)
            pool.sem_inc(stacks_cleared, 1)

            def ffn(n):
                pool.wait_ge(prefilled[n], 16)
                pool.wait_ge(slots_ready, n + 1)
                for t in range(TILES):
                    nc.gpsimd.indirect_dma_start(
                        rows_dram[n], bass.IndirectOffsetOnAxis(slot_i[:, t:t + 1].bitcast(U32), 0),
                        xn[:, t, :], None).then_inc(scattered, 16)

                def store(j, r):
                    pool.wait_ge(y_done, n * SLOT_TILES + j + 1)
                    pool.sem_inc(stores_begun, 1)
                    nc.gpsimd.indirect_dma_start(
                        y_dram[n], bass.IndirectOffsetOnAxis(slot_token[:, r:r + 1].bitcast(U32), 0),
                        yb[r % 4][:, :], None, bounds_check=TOKENS - 1, oob_is_err=False).then_inc(y_stored[r % 4], 16)

                with pool.Fori(0, SLOT_TILES // 8) as k:
                    for r in range(8):
                        store(8 * k + r, r)

            def attention():
                pool.wait_ge(xn_ready, QUADS + 1)
                nc.gpsimd.memset(mpart[:, :, :], 0.0)
                for i in range(2):
                    last = nc.gpsimd.memset(arena2[:, i], 0.0)
                pool.wait_ge(pool_own, own.done(last))

                def values(g, r):
                    src = v_all[:, bass.ds(g, 1), :].rearrange("p o (c h d) -> p (o c) h d", c=CHUNKS, h=GH)
                    nc.gpsimd.tensor_copy(v_grp[r][:, :, :, 0:HD + 1], src).then_inc(vgrp_ready, 1)

                def m_parts(u, half):
                    pool.wait_ge(smax_read, MBLOCKS * (u + 1))
                    at_least(pool, mT_ps, u)
                    m = rowmax[half][:, :]
                    zero = zeros[:, 0:MBLOCKS]
                    pool.wait_ge(pool_own, own.done(nc.gpsimd.tensor_tensor(mpart[:, 0, :], zero, m, ALU.subtract)))
                    pool.wait_ge(pool_own, own.done(nc.gpsimd.tensor_tensor(mrest[:, :], m, mpart[:, 0, :], ALU.add)))
                    pool.wait_ge(pool_own, own.done(nc.gpsimd.tensor_tensor(mpart[:, 1, :], zero, mrest[:, :], ALU.subtract)))
                    pool.wait_ge(pool_own, own.done(nc.gpsimd.tensor_tensor(mrest[:, :], mrest[:, :], mpart[:, 1, :], ALU.add)))
                    nc.gpsimd.tensor_tensor(mpart[:, 2, :], zero, mrest[:, :], ALU.subtract).then_inc(mparts_ready, 1)

                def rest(i):
                    pool.wait_ge(part0_sb, i + 1)
                    nc.gpsimd.tensor_tensor(rest_sb[i % 2], rest_sb[i % 2], part_sb[i % 4][:, 0, :],
                                            ALU.subtract).then_inc(rest_pool_ready, 1)

                def part2(i):
                    pool.wait_ge(part1_sb, i + 1)
                    nc.gpsimd.tensor_tensor(part_sb[i % 4][:, 2, :], rest_sb[i % 2], part_sb[i % 4][:, 1, :],
                                            ALU.subtract).then_inc(part2_sb, 1)

                for i in range(4):
                    part2(i)
                pool.wait_ge(v_sb, 2)
                values(0, 0)
                values(1, 1)
                for i in (4, 6):
                    rest(i)
                    rest(i + 1)
                    part2(i)
                    part2(i + 1)
                m_parts(0, 0)
                pool.wait_ge(v_act_sb, 2)
                per = 16
                start = own.n
                with pool.Fori(0, GROUPS // 2 - 1) as k:
                    own.base, own.n = start + k * per, 0
                    for s in range(4):
                        m_parts(4 * k + s + 1, (s + 1) % 2)
                        if s % 2:
                            pool.wait_ge(pv_done, 8 * (4 * k + s + 1))
                            values(2 * k + s // 2 + 2, s // 2)
                    assert own.n == per
                own.base, own.n = 0, start + per * (GROUPS // 2 - 1)
                for s in range(3):
                    m_parts(UNITS - 4 + s + 1, (s + 1) % 2)

            ffn(0)
            attention()
            ffn(1)

        @block.scalar
        def _(act):
            def transposed(use):
                act.wait_ge(var_ready, use + 1)
                nc.scalar.activation(std[:, :], var[:, :], ACT.Sqrt).then_inc(std_ready, 1)
                act.wait_ge(rstd_ready, use + 1)
                for g in range(QUADS + 1):
                    if g < QUADS:
                        t = 4 * g + 3
                        nc.scalar.activation(xn_tile(t), xres[:, t, :], ACT.Identity, scale=rstd[:, t:t + 1],
                                             bias=shift[:, t:t + 1]).then_inc(xn_act_ready, 1)
                    if g:
                        act.wait_ge(xnT_ps, use * QUADS + g)
                        nc.scalar.activation(xnT[:, (g - 1) * BANK:g * BANK], bank[(g - 1) % 2], ACT.Copy).then_inc(xnT_ready, 1)

            def ffn(n):
                transposed(2 * n)
                act.wait_ge(top_ready, n + 1)
                nc.scalar.activation(escore[:, :], top[:, :], ACT.Exp, scale=-1.0).then_inc(escore_ready, 1)
                for i in range(2 * QUADS):
                    act.wait_ge(shg_ps, 8 * n + i + 1)
                    at_least(act, shh_sb, 8 * n + i - 1)
                    nc.scalar.activation(silu_sb[i % 2], bank[5 * (i % 2)][:, :], ACT.Silu).then_inc(shsilu_sb, 1)

                base = n * SLOT_TILES

                def x_out(j, r):
                    act.wait_ge(xeT_ps, base + j + 1)
                    at_least(act, gu_ps, base + j - 1)
                    nc.scalar.activation(xeT[r % 2][:, :], bank[5 + r % 2][:, 0:P], ACT.Copy).then_inc(xeT_sb, 1)

                def silu(j, r):
                    act.wait_ge(gu_ps, base + j + 1)
                    at_least(act, h_done, base + j - 1)
                    nc.scalar.activation(silu_sb[r % 2][:, 0:INNER], bank[r % 2][:, 0:INNER], ACT.Silu).then_inc(silu_done, 1)

                def y_out(j, r):
                    act.wait_ge(y_ps, base + j + 1)
                    at_least(act, y_stored[r % 4], 4 * (base + j - r % 4))
                    nc.scalar.activation(yb[r % 4][:, :], bank[(4, 7)[r % 2]][:, 0:P], ACT.Copy).then_inc(y_done, 1)

                act.wait_ge(shh_sb, 8 * (n + 1))
                x_out(0, 0)

                def turn(j, r):
                    if not isinstance(j, int) or j + 1 < SLOT_TILES:
                        x_out(j + 1, r + 1)
                    silu(j, r)
                    if not isinstance(j, int) or j >= 3:
                        y_out(j - 3, r + 5)

                for j in range(8):
                    turn(j, j)
                with act.Fori(1, SLOT_TILES // 8 - 1) as k:
                    for r in range(8):
                        turn(8 * k + r, r)
                for j in range(SLOT_TILES - 8, SLOT_TILES):
                    turn(j, j)
                for j in range(SLOT_TILES - 3, SLOT_TILES):
                    y_out(j, j)

            def attention():
                act.wait_ge(weights_ps, 1)
                for part in range(2):
                    nc.scalar.activation(w_qkv[:, part * P:(part + 1) * P].rearrange("p (g d h) -> p g h d", g=HEADS // GH, h=GH),
                                         bank[7][:, part * P:(part + 1) * P].rearrange("p (g h d) -> p g h d", h=GH, d=HD), ACT.Copy)
                nc.scalar.activation(w_qkv[:, 2 * P:3 * P], bank[7][:, 2 * P:3 * P], ACT.Copy)
                nc.scalar.activation(w_out[:, :], bank[7][:, 3 * P:4 * P], ACT.Copy).then_inc(weights_sb, 1)
                transposed(1)

                def part0(i):
                    act.wait_ge(qk_ps, i + 1)
                    if i >= 4:
                        act.wait_ge(parts_stored[i % 4], 16 * part_stores(i))
                        act.wait_ge(part2_sb, i - 1)
                        nc.scalar.activation(rest_sb[i % 2], bank[4 + i % 4][:, :], ACT.Copy)
                    nc.scalar.activation(part_sb[i % 4][:, 0, :], bank[4 + i % 4][:, :], ACT.Copy).then_inc(part0_sb, 1)

                def part1(i):
                    if i < 4:
                        act.wait_ge(rest_ready, i + 1)
                    else:
                        act.wait_ge(rest_pool_ready, i - 3)
                    nc.scalar.activation(part_sb[i % 4][:, 1, :], rest_sb[i % 2], ACT.Copy).then_inc(part1_sb, 1)

                part0(0)
                for i in range(1, 4):
                    part0(i)
                    part1(i - 1)
                part1(3)
                for i in (4, 6):
                    part0(i)
                    part0(i + 1)
                    part1(i)
                    part1(i + 1)
                act.wait_ge(stacks_cleared, 1)
                for i in range(2, 4):
                    act.wait_ge(v_ps, i + 1)
                    src = values_src(i)
                    for g in range(HEADS // GH):
                        ins = nc.scalar.activation(values_dst(i, g), src[:, g], ACT.Copy)
                    ins.then_inc(v_act_sb, 1)

                def m_out(u):
                    act.wait_ge(mT_ps, u + 1)
                    if not (isinstance(u, int) and u == 0):
                        act.wait_ge(score_ps, STEPS * (u - 1) + 1)
                    nc.scalar.activation(mT[:, :], bank[7][0:3 * MBLOCKS, 0:P // 2].bitcast(BF16), ACT.Copy).then_inc(mT_ready, 1)

                def yT_out(g):
                    act.wait_ge(yT_ps, g + 1)
                    nc.scalar.activation(xnT[:, g * BANK:(g + 1) * BANK], bank[2], ACT.Copy).then_inc(yT_ready, 1)

                def unit(u, s, final=False):
                    for c in range(CHUNKS):
                        for h in range(GH):
                            i = c * GH + h
                            act.wait_ge(score_ps, STEPS * u + i + 1)
                            at_least(act, pv_done, CHUNKS * u + c - 1)
                            nc.scalar.activation(prob[i % 8], score_bank(i, final)[:, :], ACT.Exp, scale=SCALE).then_inc(prob_ready, 1)
                            if i == 3 and not (isinstance(u, int) and u == 0):
                                sums_out(u - 1)
                            if i == 26 and not final:
                                m_out(u + 1)
                            if final and i in (8, 12, 24):
                                yT_out({8: 0, 12: 1, 24: 2}[i])

                def sums_out(u):
                    act.wait_ge(pv_done, CHUNKS * (u + 1))
                    at_least(act, o_ps, u)
                    nc.scalar.activation(oT[:, :], bank[6], ACT.Copy).then_inc(oT_ready, 1)

                m_out(0)
                nc.scalar.activation(std[:, :], var[:, :], ACT.Exp)
                for i in range(4):
                    act.wait_ge(parts_stored[i], 32 * part_stores(i))
                for s in range(4):
                    unit(s, s)
                with act.Fori(1, GROUPS // 2 - 1) as k:
                    for s in range(4):
                        unit(4 * k + s, s)
                for s in range(4):
                    unit(UNITS - 4 + s, s, final=(s == 3))
                sums_out(UNITS - 1)
                yT_out(QUADS - 1)

            ffn(0)
            attention()
            ffn(1)

        @block.vector
        def _(dve):
            own = Tally(dve_own)

            def after(ins):
                dve.wait_ge(dve_own, own.done(ins))

            def add_projection(g):
                rows = xres[:, quad(g), :]
                dve.wait_ge(proj_ps, g + 1)
                return nc.vector.tensor_tensor(rows, rows, bank[3].rearrange("p (t h) -> p t h", h=P), ALU.add)\
                    .then_inc(proj_added, 1)

            def statistics(first, last):
                for t in range(4 * first, 4 * last):
                    ins = nc.vector.bn_stats(stats[:, t, :], xres[:, t, :])
                after(ins)
                for t in range(4 * first, 4 * last):
                    ins = nc.vector.bn_aggr(mv[:, t, :], stats[:, t, :])
                after(ins)

            def normalize(use):
                if use == 2:
                    add_projection(QUADS - 1)
                    dve.wait_ge(proj_added, QUADS)
                    statistics(QUADS - 1, QUADS)
                elif use:
                    for g in range(QUADS):
                        rows = xres[:, quad(g), :]
                        dve.wait_ge(y_loaded[g], 16 * ((use + 1) // 2))
                        ins = nc.vector.scalar_tensor_tensor(out=rows, in0=y_back[:, quad(g), :], scalar=0.5, in1=rows,
                                                             op0=ALU.mult, op1=ALU.add)
                        if use == 3:
                            ins.then_inc(out_ready, 1)
                    if use == 3:
                        return
                    after(ins)
                    statistics(0, QUADS)
                else:
                    for g in range(QUADS):
                        dve.wait_ge(x_loaded[g], 16)
                        statistics(g, g + 1)
                nc.vector.tensor_scalar(var[:, :], mv[:, :, 1], EPS, None, ALU.add).then_inc(var_ready, 1)
                dve.wait_ge(std_ready, use + 1)
                after(nc.vector.reciprocal(rstd[:, :], std[:, :]))
                after(nc.vector.tensor_tensor(newton[:, :], rstd[:, :], rstd[:, :], ALU.mult))
                after(nc.vector.tensor_tensor(newton[:, :], newton[:, :], var[:, :], ALU.mult))
                after(nc.vector.tensor_scalar(newton[:, :], newton[:, :], -0.5, 1.5, ALU.mult, ALU.add))
                after(nc.vector.tensor_tensor(rstd[:, :], rstd[:, :], newton[:, :], ALU.mult))
                nc.vector.scalar_tensor_tensor(out=shift[:, :], in0=mv[:, :, 0], scalar=-1.0, in1=rstd[:, :],
                                               op0=ALU.mult, op1=ALU.mult).then_inc(rstd_ready, 1)
                if use == 2:
                    dve.wait_ge(yT_ps, QUADS)
                for g in range(QUADS):
                    for t in range(4 * g, 4 * g + 3):
                        ins = nc.vector.tensor_scalar(xn_tile(t), xres[:, t, :], mv[:, t, 0:1], rstd[:, t:t + 1],
                                                      ALU.subtract, ALU.mult)
                    ins.then_inc(xn_ready, 1)

            def ffn(n):
                dve.wait_ge(consts_ready, 2)
                normalize(2 * n)
                logits = bank[2].rearrange("p (t e) -> p t e", e=EXPERTS)
                wide = lambda a: a.unsqueeze(2).broadcast_to([P, TILES, EXPERTS])
                rev3 = rev[:, :].unsqueeze(1).broadcast_to([P, TILES, EXPERTS])
                dve.wait_ge(logits_ready, n + 1)
                ins = nc.vector.tensor_reduce(top[:, :], logits, AX_X, ALU.max)
                ins.then_inc(top_ready, 1)
                dve.wait_ge(top_ready, n + 1)
                after(nc.vector.tensor_tensor(hit, logits, wide(top[:, :]), ALU.is_equal))
                after(nc.vector.tensor_tensor(cand, hit, rev3, ALU.mult))
                after(nc.vector.tensor_reduce(rtop[:, :], cand, AX_X, ALU.max))
                nc.vector.tensor_tensor(onehot3, rev3, wide(rtop[:, :]), ALU.is_equal).then_inc(onehot_ready, 1)

                def sh_product(i):
                    dve.wait_ge(shsilu_sb, 8 * n + i + 1)
                    at_least(dve, shy_ps, 4 * n + i // 2 - 1)
                    nc.vector.tensor_tensor(h_sh[i // 2 % 2][i % 2], bank[1 + 5 * (i % 2)][:, :], silu_sb[i % 2],
                                            ALU.mult).then_inc(shh_sb, 1)

                def sh_add(q):
                    dve.wait_ge(shy_ps, 4 * n + q + 1)
                    nc.vector.scalar_tensor_tensor(out=xres[:, quad(q), :], in0=bank[7].rearrange("p (t h) -> p t h", h=P),
                                                   scalar=0.5, in1=xres[:, quad(q), :], op0=ALU.mult, op1=ALU.add)\
                        .then_inc(shy_added, 1)

                dve.wait_ge(escore_ready, n + 1)
                after(nc.vector.tensor_scalar(escore[:, :], escore[:, :], 1.0, None, ALU.add))
                after(nc.vector.reciprocal(score[:, :], escore[:, :]))
                sh_product(0)
                after(nc.vector.tensor_tensor(xn[:, :, 0:P], xn[:, :, 0:P], score[:, :].unsqueeze(2).broadcast_to([P, TILES, P]), ALU.mult))
                dve.wait_ge(ranks_ready, n + 1)
                count = bank[4][:, 0:EXPERTS]
                after(nc.vector.tensor_scalar(count_i[:, :], count, float(P - 1), None, ALU.add))
                after(nc.vector.tensor_scalar(count_i[:, :], count_i[:, :], 7, 7, ALU.logical_shift_right, ALU.logical_shift_left))
                after(nc.vector.tensor_copy(slots_of[:, :], count_i[:, :]))
                after(nc.vector.tensor_tensor_scan(slots_to[:, :], slots_of[:, :], zeros[:, :], 0.0, ALU.add, ALU.add))
                after(nc.vector.tensor_tensor(base_e[:, :], slots_to[:, :], slots_of[:, :], ALU.subtract))
                after(nc.vector.tensor_tensor(place, bank[3].rearrange("p (t e) -> p t e", e=EXPERTS),
                                              base_e[:, :].unsqueeze(1).broadcast_to([P, TILES, EXPERTS]), ALU.add))
                after(nc.vector.tensor_tensor(place, place, onehot3, ALU.mult))
                after(nc.vector.tensor_reduce(slot_f[:, :], place, AX_X, ALU.add))
                nc.vector.tensor_copy(slot_i[:, :], slot_f[:, :]).then_inc(slots_ready, 1)
                after(nc.vector.tensor_scalar(below[:, :], slots_to[:, :], 1.0 / P, None, ALU.mult))
                after(nc.vector.tensor_scalar(below[:, :], below[:, :], slot_tile[:, 0:1], None, ALU.is_le))
                after(nc.vector.tensor_reduce(eid[:, :], below[:, :], AX_X, ALU.add))
                nc.vector.tensor_scalar(eid[:, :], eid[:, :], float(EXPERTS - 1), float(WROW), ALU.min, ALU.mult).then_inc(eid_ready, 1)
                sh_product(1)
                dve.wait_ge(eid_row, n + 1)
                nc.vector.tensor_copy(woff[:, :], bank[4][0:1, P:2 * P]).then_inc(woff_ready, 1)
                sh_product(2)
                sh_product(3)
                sh_add(0)
                sh_product(4)
                sh_product(5)
                sh_add(1)
                sh_product(6)
                sh_product(7)
                sh_add(2)
                sh_add(3)

                base = n * SLOT_TILES

                def hT_out(j, r):
                    dve.wait_ge(hT_ps, base + j + 1)
                    at_least(dve, y_ps, base + j - 1)
                    nc.vector.tensor_copy(hT_sb[r % 2], bank[2 + r % 2][:, 0:INNER]).then_inc(hT_done, 1)

                def product(j, r):
                    dve.wait_ge(silu_done, base + j + 1)
                    at_least(dve, hT_ps, base + j - 1)
                    nc.vector.tensor_tensor(h_sb[r % 2], bank[r % 2][:, INNER:2 * INNER], silu_sb[r % 2][:, 0:INNER],
                                            ALU.mult).then_inc(h_done, 1)

                def ids(j, r):
                    dve.wait_ge(xe_loaded[r % 4], 4 * (base + j - r % 4) + 16)
                    at_least(dve, y_stored[r % 4], 4 * (base + j - r % 4) - 16)
                    nc.vector.tensor_copy(slot_token[:, r % 8:r % 8 + 1], xe[r % 4][:, P:P + 1].bitcast(I32)).then_inc(ids_done, 1)

                def turn(j, r):
                    product(j, r)
                    if not isinstance(j, int) or j >= 2:
                        hT_out(j - 2, r)
                    if not isinstance(j, int) or j + 1 < SLOT_TILES:
                        ids(j + 1, r + 1)

                ids(0, 0)
                for j in range(8):
                    turn(j, j)
                with dve.Fori(1, SLOT_TILES // 8 - 1) as k:
                    for r in range(8):
                        turn(8 * k + r, r)
                for j in range(SLOT_TILES - 8, SLOT_TILES):
                    turn(j, j)
                for j in range(SLOT_TILES - 2, SLOT_TILES):
                    hT_out(j, j)

            def attention():
                normalize(1)
                for i in range(4):
                    dve.wait_ge(part0_sb, i + 1)
                    at_least(dve, part2_sb, i - 1)
                    nc.vector.tensor_tensor(rest_sb[i % 2], bank[4 + i % 4][:, :], part_sb[i % 4][:, 0, :],
                                            ALU.subtract).then_inc(rest_ready, 1)
                dve.wait_ge(stacks_cleared, 1)
                for i in range(2):
                    dve.wait_ge(v_ps, i + 1)
                    src = values_src(i)
                    for g in range(HEADS // GH):
                        ins = nc.vector.tensor_copy(values_dst(i, g), src[:, g])
                    ins.then_inc(v_sb, 1)

                def row_max(u, m):
                    i = MBLOCKS * u[0] + m
                    dve.wait_ge(smax_ps, i + 1)
                    at_least(dve, mparts_ready, u[0] - 1)
                    nc.vector.tensor_reduce(rowmax[u[1] % 2][:, m:m + 1], pair[m % 2][:, :], AX_X, ALU.max).then_inc(smax_read, 1)

                def store_norm(u, b, g, half):
                    dve.wait_ge(o_ps, u + 1)
                    o = bank[7].rearrange("p (t h d) -> p t h d", t=4, h=GH)
                    after(nc.vector.reciprocal(rden[:, :, :], o[:, :, :, HD]))
                    t0 = 8 * b + 4 * half
                    for t in range(4):
                        dst = xn[:, bass.ds(t0 + t, 1), bass.ds(g * GH * HD, GH * HD)].rearrange("p o (h d) -> p (o h) d", d=HD)
                        ins = nc.vector.tensor_tensor(dst, o[:, t, :, 0:HD],
                                                      rden[:, t, :].unsqueeze(2).broadcast_to([P, GH, HD]), ALU.mult)
                    ins.then_inc(o_normed, 1)

                def unit(u, s, b, g, first=False, last=9):
                    for c, blocks in enumerate(MAXIMA):
                        for ahead, m in blocks:
                            if ahead < last:
                                row_max((u + ahead, s + ahead), m)
                        if c == 2 and not first:
                            store_norm(u - 1, b, g, (s + 1) % 2)

                for m in range(MBLOCKS):
                    row_max((0, 0), m)
                for m in range(AHEAD):
                    row_max((1, 1), m)
                unit(0, 0, 0, 0, first=True)
                for s in range(1, 4):
                    unit(s, s, 0, (s - 1) // 2)
                start = own.n
                per = 4
                with dve.Fori(1, GROUPS // 2 - 1) as k:
                    own.base, own.n = start + (k - 1) * per, 0
                    unit(4 * k, 0, 0, 2 * k - 1)
                    for s in range(1, 4):
                        unit(4 * k + s, s, k - 1, 4 - 2 * k + (s - 1) // 2)
                    assert own.n == per
                own.base, own.n = 0, start + per * (GROUPS // 2 - 2)
                unit(UNITS - 4, 0, 1, 1)
                unit(UNITS - 3, 1, 1, 2)
                unit(UNITS - 2, 2, 1, 2, last=2)
                unit(UNITS - 1, 3, 1, 3, last=1)
                for g in range(QUADS - 1):
                    add_projection(g)
                    dve.wait_ge(proj_added, g + 1)
                    statistics(g, g + 1)
                store_norm(UNITS - 1, 1, 3, 1)

            ffn(0)
            attention()
            ffn(1)
            normalize(3)

        @block.tensor
        def _(pe):
            pe.wait_ge(consts_ready, 2)

            def transposes(use, beside=None):
                for g in range(QUADS):
                    pe.wait_ge(xn_ready, use * QUADS + g + 1)
                    pe.wait_ge(xn_act_ready, use * QUADS + g + 1)
                    at_least(pe, xnT_ready, use * QUADS + g - 1)
                    for t in range(4):
                        ins = nc.tensor.transpose(bank[g % 2][:, t * P:(t + 1) * P], xn_tile(4 * g + t), identf[:, :])
                    ins.then_inc(xnT_ps, 1)
                    if beside and g:
                        beside(g - 1)
                if beside:
                    beside(QUADS - 1)

            def ffn(n):
                def logits(g):
                    if n == 0 and g == 0:
                        pe.wait_ge(small_loaded, 16 * 8)
                    pe.wait_ge(xnT_ready, 2 * n * QUADS + g + 1)
                    for t in range(4 * g, 4 * g + 4):
                        ins = nc.tensor.matmul(bank[2][:, t * EXPERTS:(t + 1) * EXPERTS], xnT[:, t * P:(t + 1) * P], gate_sb[:, :],
                                               start=True, stop=True)
                    if g == QUADS - 1:
                        ins.then_inc(logits_ready, 1)

                transposes(2 * n, logits)

                def sh_up(i):
                    q, c = i // 2, i % 2
                    at_least(pe, shh_sb, 8 * n + i - 1)
                    for part, b in ((0, bank[5 * c]), (INNER, bank[1 + 5 * c])):
                        ins = nc.tensor.matmul(b[:, :], w_sh[:, part + c * P:part + (c + 1) * P], xnT[:, q * BANK:(q + 1) * BANK],
                                               start=True, stop=True)
                    ins.then_inc(shg_ps, 1)

                def sh_down(q):
                    pe.wait_ge(shh_sb, 8 * n + 2 * q + 2)
                    at_least(pe, shy_added, 4 * n + q)
                    for t in range(4):
                        for c in range(2):
                            ins = nc.tensor.matmul(bank[7][:, t * P:(t + 1) * P], h_sh[q % 2][c][:, t * P:(t + 1) * P],
                                                   w_sh[:, 2 * INNER + c * P:2 * INNER + (c + 1) * P], start=(c == 0), stop=(c == 1))
                    ins.then_inc(shy_ps, 1)

                sh_up(0)
                pe.wait_ge(onehot_ready, n + 1)
                for t in range(TILES):
                    nc.tensor.matmul(bank[4][:, 0:EXPERTS], onesb[:, :], onehot[:, t * EXPERTS:(t + 1) * EXPERTS],
                                     start=(t == 0), stop=(t == TILES - 1))
                nc.tensor.matmul(bank[3], before[:, :], onehot, start=True, stop=False)
                for d in range(1, TILES):
                    ins = nc.tensor.matmul(bank[3][:, d * EXPERTS:], onesb[:, :], onehot[:, 0:(TILES - d) * EXPERTS],
                                           start=False, stop=(d == TILES - 1))
                ins.then_inc(ranks_ready, 1)
                sh_up(1)
                sh_up(2)
                pe.wait_ge(eid_ready, n + 1)
                nc.tensor.matmul(bank[4][0:1, P:2 * P], eid[:, :], identf[:, :], start=True, stop=True).then_inc(eid_row, 1)
                sh_up(3)
                sh_down(0)
                sh_up(4)
                sh_up(5)
                sh_down(1)
                sh_up(6)
                sh_up(7)
                sh_down(2)
                sh_down(3)

                base = n * SLOT_TILES

                def x_transpose(j, r):
                    pe.wait_ge(xe_loaded[r % 4], 4 * (base + j - r % 4) + 16)
                    at_least(pe, xeT_sb, base + j - 1)
                    nc.tensor.transpose(bank[5 + r % 2][:, 0:P], xe[r % 4][:, 0:P], identf[:, :]).then_inc(xeT_ps, 1)

                def weights_of(j):
                    return pe.value_load(woff[0:1, bass.ds(j, 1)], min_val=0, max_val=(EXPERTS - 1) * WROW)

                def gate_up(j, r, e):
                    pe.wait_ge(xeT_sb, base + j + 1)
                    at_least(pe, h_done, base + j - 1)
                    nc.tensor.matmul(bank[r % 2][:, :], xeT[r % 2][:, :], w_exp[:, bass.ds(e, 2 * INNER)],
                                     start=True, stop=True).then_inc(gu_ps, 1)

                def h_transpose(j, r):
                    pe.wait_ge(h_done, base + j + 1)
                    at_least(pe, hT_done, base + j - 1)
                    for c in range(2):
                        ins = nc.tensor.transpose(bank[2 + r % 2][:, c * P:(c + 1) * P], h_sb[r % 2][:, c * P:(c + 1) * P], identf[:, :])
                    ins.then_inc(hT_ps, 1)

                def down(j, r, e):
                    pe.wait_ge(hT_done, base + j + 1)
                    at_least(pe, y_done, base + j - 1)
                    for c in range(2):
                        ins = nc.tensor.matmul(bank[(4, 7)[r % 2]][:, 0:P], hT_sb[r % 2][:, c * P:(c + 1) * P],
                                               w_exp[:, bass.ds(e + 2 * INNER + c * P, P)], start=(c == 0), stop=(c == 1))
                    ins.then_inc(y_ps, 1)

                pe.wait_ge(woff_ready, n + 1)
                pe.wait_ge(experts_loaded, 16 * 16)
                pe.wait_ge(shy_added, 4 * (n + 1))

                def turns(j0, first=False, last=False):
                    e = {r: weights_of(j0 + r) for r in ((0,) if first else (-3, -2, -1, 0))}
                    for r in range(8):
                        if not (last and r == 7):
                            x_transpose(j0 + r + 1, r + 1)
                        gate_up(j0 + r, r, e[r])
                        if r < 7:
                            e[r + 1] = weights_of(j0 + r + 1)
                        if not first or r >= 2:
                            h_transpose(j0 + r - 2, r)
                        if not first or r >= 3:
                            down(j0 + r - 3, r + 1, e[r - 3])
                    if last:
                        h_transpose(j0 + 6, 0)
                        down(j0 + 5, 1, e[5])
                        h_transpose(j0 + 7, 1)
                        down(j0 + 6, 0, e[6])
                        down(j0 + 7, 1, e[7])

                x_transpose(0, 0)
                turns(0, first=True)
                with pe.Fori(1, SLOT_TILES // 8 - 1) as k:
                    turns(8 * k)
                turns(SLOT_TILES - 8, last=True)

            def attention():
                pe.wait_ge(y_done, SLOT_TILES)
                nc.tensor.matmul(bank[7][:, 0:3 * P], wv_sb[:, :], wut_sb[:, :], start=True, stop=True)
                nc.tensor.matmul(bank[7][:, 3 * P:4 * P], wov_sb[:, :], wout_sb[:, :], start=True, stop=True).then_inc(weights_ps, 1)
                transposes(1)
                pe.wait_ge(weights_sb, 1)

                def project_qk(i):
                    b, qk, half = i // 4, i // 2 % 2, i % 2
                    pe.wait_ge(xnT_ready, QUADS + 2 * b + half + 1)
                    at_least(pe, rest_ready, i - 3)
                    nc.tensor.matmul(bank[4 + i % 4][:, :], w_qkv[:, qk * P:(qk + 1) * P],
                                     xnT[:, (2 * b + half) * BANK:(2 * b + half + 1) * BANK], start=True, stop=True).then_inc(qk_ps, 1)

                def project_v(i):
                    for c in range(4):
                        t = 4 * i + c
                        ins = nc.tensor.matmul(v_bank(i)[:, c * P:(c + 1) * P], xnT[:, t * P:(t + 1) * P],
                                               w_qkv[:, 2 * P:3 * P], start=True, stop=True)
                    ins.then_inc(v_ps, 1)

                for i in range(4):
                    project_qk(i)
                project_v(0)
                project_v(1)
                for i in range(4, 8):
                    project_qk(i)
                pe.wait_ge(v_sb, 2)

                def max_scores(u, m, part):
                    h, t, i = m // 4, m % 4, MBLOCKS * u[0] + m
                    r, half = u[1] // 2 % 2, u[1] % 2
                    if part == 0:
                        at_least(pe, smax_read, i - 1)
                    ins = nc.tensor.matmul(pair[m % 2][:, part * BANK:(part + 1) * BANK], q_stack[r][0:MROW, half, h, t * P:(t + 1) * P],
                                           k_stack[r][0:MROW, h, part * BANK:(part + 1) * BANK], start=True, stop=True)
                    if part == 1:
                        ins.then_inc(smax_ps, 1)

                def scores(u, s, i, final):
                    c, h, r, half = i // GH, i % GH, s // 2 % 2, s % 2
                    at_least(pe, prob_ready, STEPS * u + i - (3 if final and i >= 2 else 1))
                    nc.tensor.matmul(score_bank(i, final)[:, :], k_stack[r][:, h, c * P:(c + 1) * P],
                                     q_stack[r][:, half, h, :], start=True, stop=True).then_inc(score_ps, 1)

                def weigh(u, s, c):
                    pe.wait_ge(prob_ready, STEPS * u + GH * (c + 1))
                    if c == 0:
                        at_least(pe, oT_ready, u)
                    for h in range(GH):
                        ins = nc.tensor.matmul(bank[6][32 * h:32 * (h + 1), :], v_grp[s // 2 % 2][:, c, h, :], prob[(c * GH + h) % 8],
                                               start=(c == 0), stop=(c == CHUNKS - 1))
                    ins.then_inc(pv_done, 1)

                def o_transpose(u):
                    pe.wait_ge(oT_ready, u + 1)
                    at_least(pe, o_normed, u)
                    pe.wait_ge(mT_ready, UNITS if isinstance(u, int) and u + 2 > UNITS else u + 2)
                    for t in range(4):
                        ins = nc.tensor.transpose(bank[7][:, t * P:(t + 1) * P], oT[:, t * P:(t + 1) * P], identf[:, :])
                    ins.then_inc(o_ps, 1)

                def m_transpose(u):
                    pe.wait_ge(mparts_ready, u + 1)
                    at_least(pe, o_normed, u - 1)
                    nc.tensor.transpose(bank[7][:, 0:P // 2].bitcast(BF16),
                                        mpart[:, :, :].rearrange("p c m -> p (c m)"), identb[:, :]).then_inc(mT_ps, 1)

                def out_transpose(g):
                    if g >= 2:
                        pe.wait_ge(o_normed, UNITS - QUADS + g + 1)
                    pe.wait_ge(smax_read, UNITS * MBLOCKS)
                    at_least(pe, yT_ready, g)
                    for t in range(4):
                        ins = nc.tensor.transpose(bank[2][:, t * P:(t + 1) * P], xn_tile(4 * g + t), identf[:, :])
                    ins.then_inc(yT_ps, 1)

                def project_out(g):
                    pe.wait_ge(yT_ready, g + 1)
                    at_least(pe, proj_added, g)
                    for t in range(4):
                        at = (4 * g + t) * P
                        ins = nc.tensor.matmul(bank[3][:, t * P:(t + 1) * P], xnT[:, at:at + P], w_out[:, :], start=True, stop=True)
                    ins.then_inc(proj_ps, 1)

                def unit(u, s, quarter, first=False, last=9):
                    if s % 2 == 0:
                        pe.wait_ge(vgrp_ready, 2 * quarter + s // 2 + 1)
                    pe.wait_ge(m_loaded[s % 2], 48 * (2 * quarter + s // 2 + 1))

                    def values_before(c):
                        if c:
                            weigh(u, s, c - 1)
                        elif not first:
                            weigh(u - 1, s - 1 + 4, CHUNKS - 1)

                    next_group = s % 2 == 0
                    for c, blocks in enumerate(MAXIMA):
                        blocks = [b for b in blocks if b[0] < last]
                        scores(u, s, GH * c, last == 1)
                        scores(u, s, GH * c + 1, last == 1)
                        for ahead, m in blocks:
                            if ahead == 2 and next_group:
                                pe.wait_ge(stack_loaded[(s // 2 + 1) % 2], 16 * 6 * (quarter + (s + 2) // 4 + 1))
                                next_group = False
                            max_scores((u + ahead, s + ahead), m, 0)
                            max_scores((u + ahead, s + ahead), m, 1)
                        if c == 6 and last > 1:
                            m_transpose(u + 1)
                        if not blocks:
                            values_before(c)
                        scores(u, s, GH * c + 2, last == 1)
                        scores(u, s, GH * c + 3, last == 1)
                        if blocks:
                            values_before(c)
                        if c == 2 and not first:
                            o_transpose(u - 1)
                        if last == 1:
                            if c in (2, 3, 6):
                                project_out({2: 0, 3: 1, 6: 2}[c])
                            if c in (1, 2, 5):
                                out_transpose({1: 0, 2: 1, 5: 2}[c])

                pe.wait_ge(stack_loaded[0], 16 * 6)
                for m in range(MBLOCKS):
                    for part in range(2):
                        max_scores((0, 0), m, part)
                    if m in (8, 9):
                        pe.wait_ge(part0_sb, m - 1)
                        project_v(m - 6)
                pe.wait_ge(v_act_sb, 2)
                for m in range(AHEAD):
                    for part in range(2):
                        max_scores((1, 1), m, part)
                    if m == 2:
                        m_transpose(0)
                for s in range(4):
                    unit(s, s, 0, first=(s == 0))
                with pe.Fori(1, GROUPS // 2 - 1) as k:
                    for s in range(4):
                        unit(4 * k + s, s, k)
                for s in range(4):
                    unit(UNITS - 4 + s, s, GROUPS // 2 - 1, last=(9, 9, 2, 1)[s])
                weigh(UNITS - 1, 3, CHUNKS - 1)
                o_transpose(UNITS - 1)

                out_transpose(QUADS - 1)
                project_out(QUADS - 1)

            ffn(0)
            attention()
            ffn(1)


_ORDER = ["x", "w_qkv_v", "w_qkv_ut", "w_o_v", "w_o_ut", "gate_w", "sh_gate", "sh_up", "sh_down", "r_gate", "r_up", "r_down"]


def kernel(L0_attn_x, L0_attn_W_qkv_v, L0_attn_W_qkv_u, L0_attn_W_o_v, L0_attn_W_o_u, L0_ffn_gate_w,
           L0_ffn_shared_gate_w, L0_ffn_shared_up_w, L0_ffn_shared_down_w, L0_ffn_routed_gate_w,
           L0_ffn_routed_up_w, L0_ffn_routed_down_w):
    import numpy as np
    import concourse.bacc as bacc
    from concourse.bass_utils import run_bass_kernel_spmd

    arrays = [L0_attn_x, L0_attn_W_qkv_v, np.asarray(L0_attn_W_qkv_u).T, L0_attn_W_o_v, np.asarray(L0_attn_W_o_u).T,
              L0_ffn_gate_w, L0_ffn_shared_gate_w, L0_ffn_shared_up_w, L0_ffn_shared_down_w, L0_ffn_routed_gate_w,
              L0_ffn_routed_up_w, L0_ffn_routed_down_w]
    nc = bacc.Bacc("TRN2", target_bir_lowering=False, num_devices=1)
    given, args = {}, []
    for name, a in zip(_ORDER, arrays):
        a = np.ascontiguousarray(a)
        given[f"in_{name}"] = a
        args.append(nc.dram_tensor(f"in_{name}", a.shape, mybir.dt.from_np(a.dtype), kind="ExternalInput").ap())
    out = nc.dram_tensor("out", given["in_x"].shape, F32, kind="ExternalOutput").ap()
    build(nc, *args, out)
    return run_bass_kernel_spmd(nc, [given], core_ids=[0]).results[0]["out"]
```

```python
from contextlib import ExitStack

import concourse.bass as bass
from concourse import mybir

F32 = mybir.dt.float32
BF16 = mybir.dt.bfloat16
I32 = mybir.dt.int32
U32 = mybir.dt.uint32
ALU = mybir.AluOpType
ACT = mybir.ActivationFunctionType
AX_X = mybir.AxisListType.X

P = 128
BANK = 512
TILES = 16
QUADS = TILES // 4
TOKENS = TILES * P
EXPERTS = 32
INNER = 256
WROW = 3 * INNER
SLOT_TILES = (TOKENS + EXPERTS * (P - 1)) // P
LAST_TILES = SLOT_TILES // 8 * 8
ROW = P + 4
NOWHERE = 4 * TOKENS
EPS = 1e-5
RSQRT_SEED = 0x5F3759DF
NEWTON_STEPS = 3

HEADS = 16
HD = 8
SEQ = 1024
GH = 4
GROUPS = 2 * HEADS // GH
UNITS = 2 * GROUPS
CHUNKS = SEQ // P
QW = 512
STEPS = CHUNKS * GH
AHEAD = 6
MBLOCKS = GH * QW // P
Q_OF_K = (3, 2, 1)
STACK_LOADS = 2 * len(Q_OF_K)
MROW = 96
SCALE = float(HD) ** -0.5


class Tally:

    def __init__(self, sem):
        self.sem, self.base, self.n = sem, 0, 0

    def done(self, ins):
        ins.then_inc(self.sem, 1)
        self.n += 1
        return self.base + self.n


ORDER = [(1, m) for m in range(AHEAD, MBLOCKS)] + [(2, m) for m in range(AHEAD)]
MAXIMA = [ORDER[2 * c:2 * c + 2] for c in range(CHUNKS)]


def ring_signals(n, j, r):
    tiles_per_ffn = len(range(r % 4, SLOT_TILES, 4))
    return 16 * n * tiles_per_ffn + 4 * (j - r % 4)


def at_least(eng, sem, value):
    if not isinstance(value, int) or value > 0:
        eng.wait_ge(sem, value)


def build(nc, x_in, w_qkv_v, w_qkv_ut, w_o_v, w_o_ut, gate_w, sh_gate, sh_up, sh_down, r_gate, r_up, r_down, out):
    x_view = x_in.rearrange("b (t p) h -> p (b t) h", p=P)
    out_view = out.rearrange("b (t p) h -> p (b t) h", p=P)

    with ExitStack() as ctx:
        def sb(name, shape, dt=F32):
            return ctx.enter_context(nc.sbuf_tensor(name, shape, dt))

        def sem(name):
            return ctx.enter_context(nc.semaphore(name))

        rows_dram = [nc.dram_tensor(f"rows{n}", (SLOT_TILES * P, ROW), F32, kind="Internal").ap() for n in range(2)]
        y_dram = [nc.dram_tensor(f"y{n}", (TOKENS, P), F32, kind="Internal").ap() for n in range(2)]
        q_dram = nc.dram_tensor("q_parts", (3, 2 * P // GH, GH * SEQ), BF16, kind="Internal").ap()
        k_dram = nc.dram_tensor("k_parts", (3, 2 * P, SEQ), BF16, kind="Internal").ap()

        pair = [ctx.enter_context(nc.psum_tensor(f"pair{i}", [P, 2 * BANK], F32)) for i in range(2)]
        bank = [pair[i // 2][:, i % 2 * BANK:(i % 2 + 1) * BANK] for i in range(4)]
        bank += [ctx.enter_context(nc.psum_tensor(f"bank{i}", [P, BANK], F32))[:, :] for i in range(4, 8)]

        w_exp = sb("w_exp", [P, EXPERTS * WROW])
        w_sh = sb("w_sh", [P, WROW])
        gate_sb = sb("gate_sb", [P, EXPERTS])
        wv_sb = sb("wv_sb", [32, P])
        wut_sb = sb("wut_sb", [32, 3 * P])
        wov_sb = sb("wov_sb", [32, P])
        wout_sb = sb("wout_sb", [32, P])
        w_qkv = sb("w_qkv", [P, 3 * P])
        w_out = sb("w_out", [P, P])

        xres = sb("xres", [P, TILES, P])
        xn = sb("xn", [P, TILES, ROW])
        xnT = sb("xnT", [P, TOKENS])
        y_back = xnT[:, :].rearrange("p (t h) -> p t h", h=P)

        identf = sb("identf", [P, P])
        identb = sb("identb", [P, P], BF16)
        before = sb("before", [P, P], BF16)
        onesb = sb("onesb", [P, P], BF16)
        iota_i = sb("iota_i", [P, EXPERTS], I32)
        rev = sb("rev", [P, EXPERTS])
        slot_tile_i = sb("slot_tile_i", [P, 1], I32)
        slot_tile = sb("slot_tile", [P, 1])
        zeros = sb("zeros", [P, EXPERTS])
        empty_row = sb("empty_row", [P, ROW])

        stats = sb("stats", [P, TILES, 6])
        mv = sb("mv", [P, TILES, 2])
        var = sb("var", [P, TILES])
        seed = sb("seed", [P, TILES], I32)
        rstd = sb("rstd", [P, TILES])
        newton = sb("newton", [P, TILES])
        shift = sb("shift", [P, TILES])
        top = sb("top", [P, TILES])
        rtop = sb("rtop", [P, TILES])
        escore = sb("escore", [P, TILES])
        score = sb("score", [P, TILES])
        count_i = sb("count_i", [P, EXPERTS], I32)
        slots_of = sb("slots_of", [P, EXPERTS])
        slots_to = sb("slots_to", [P, EXPERTS])
        base_e = sb("base_e", [P, EXPERTS])
        below = sb("below", [P, EXPERTS])
        eid = sb("eid", [P, 1])
        slot_f = sb("slot_f", [P, TILES])
        slot_i = sb("slot_i", [P, TILES], I32)
        woff = sb("woff", [1, P], I32)

        xe = [sb(f"xe{i}", [P, ROW]) for i in range(4)]
        xeT = [sb(f"xeT{i}", [P, P]) for i in range(2)]
        yb = [sb(f"yb{i}", [P, P]) for i in range(4)]
        slot_token = sb("slot_token", [P, 8], I32)

        arena = sb("arena", [P, 8 * BANK])
        silu_sb = [arena[:, i * BANK:(i + 1) * BANK] for i in range(2)]
        h_sh = [[arena[:, (2 + 2 * i + c) * BANK:(3 + 2 * i + c) * BANK] for c in range(2)] for i in range(2)]
        h_sb = [arena[:, 6 * BANK + i * INNER:6 * BANK + (i + 1) * INNER] for i in range(2)]
        hT_sb = [arena[:, 7 * BANK + i * INNER:7 * BANK + (i + 1) * INNER] for i in range(2)]
        part_sb = [arena[:, i * 768:(i + 1) * 768].bitcast(BF16).rearrange("p (c t) -> p c t", c=3) for i in range(4)]
        rest_sb = [arena[:, (6 + i) * BANK:(7 + i) * BANK] for i in range(2)]
        prob = [arena[:, i * BANK:(i + 1) * BANK] for i in range(8)]

        arena2 = sb("arena2", [P, 2, CHUNKS, GH, 32])
        flat2 = arena2[:, :, :, :, :].rearrange("p a c h d -> p (a c h d)")
        hit = flat2[:, 0:512].rearrange("p (t e) -> p t e", e=EXPERTS)
        cand = flat2[:, 512:1024].rearrange("p (t e) -> p t e", e=EXPERTS)
        place = flat2[:, 1024:1536].rearrange("p (t e) -> p t e", e=EXPERTS)
        onehot = flat2[:, 1536:1792].bitcast(BF16)
        onehot3 = onehot.rearrange("p (t e) -> p t e", e=EXPERTS)
        v_grp = [arena2[:, i] for i in range(2)]

        v_all = sb("v_all", [P, GROUPS, CHUNKS * GH * (HD + 1)])
        v_all5 = v_all[:, :, :].rearrange("p g (c h d) -> p g c h d", c=CHUNKS, h=GH)
        q_stack = [sb(f"q_stack{i}", [P, 2, GH, QW], BF16) for i in range(2)]
        k_stack = [sb(f"k_stack{i}", [P, GH, SEQ], BF16) for i in range(2)]
        rowmax = [sb(f"rowmax{i}", [P, MBLOCKS]) for i in range(2)]
        mrest = sb("mrest", [P, MBLOCKS])
        mpart = sb("mpart", [P, P // MBLOCKS, MBLOCKS], BF16)
        mT = sb("mT", [3 * MBLOCKS, P], BF16)
        oT = sb("oT", [P, QW])
        rden = sb("rden", [P, 4, GH])

        x_loaded = [sem(f"x_loaded{g}") for g in range(QUADS)]
        small_loaded = sem("small_loaded")
        experts_loaded = sem("experts_loaded")
        consts_ready = sem("consts_ready")
        stacks_cleared = sem("stacks_cleared")
        prefilled = [sem(f"prefilled{n}") for n in range(2)]
        weights_ps = sem("weights_ps")
        weights_sb = sem("weights_sb")
        dve_own = sem("dve_own")
        pool_own = sem("pool_own")
        rstd_ready = sem("rstd_ready")
        xn_ready = sem("xn_ready")
        xn_act_ready = sem("xn_act_ready")
        out_ready = sem("out_ready")
        xnT_ps = sem("xnT_ps")
        xnT_ready = sem("xnT_ready")
        logits_ready = sem("logits_ready")
        top_ready = sem("top_ready")
        escore_ready = sem("escore_ready")
        onehot_ready = sem("onehot_ready")
        ranks_ready = sem("ranks_ready")
        eid_ready = sem("eid_ready")
        eid_row = sem("eid_row")
        woff_ready = sem("woff_ready")
        slots_ready = sem("slots_ready")
        scattered = sem("scattered")
        shg_ps = sem("shg_ps")
        shsilu_sb = sem("shsilu_sb")
        shh_sb = sem("shh_sb")
        shy_ps = sem("shy_ps")
        shy_added = sem("shy_added")
        xe_loaded = [sem(f"xe_loaded{i}") for i in range(4)]
        xeT_ps = sem("xeT_ps")
        xeT_sb = sem("xeT_sb")
        gu_ps = sem("gu_ps")
        silu_done = sem("silu_done")
        h_done = sem("h_done")
        hT_ps = sem("hT_ps")
        hT_done = sem("hT_done")
        y_ps = sem("y_ps")
        y_done = sem("y_done")
        ids_done = sem("ids_done")
        y_stored = [sem(f"y_stored{i}") for i in range(4)]
        stores_begun = sem("stores_begun")
        y_loaded = [sem(f"y_loaded{g}") for g in range(QUADS)]
        qk_ps = sem("qk_ps")
        part0_sb = sem("part0_sb")
        rest_ready = sem("rest_ready")
        rest_pool_ready = sem("rest_pool_ready")
        part1_sb = sem("part1_sb")
        part2_sb = sem("part2_sb")
        parts_stored = [sem(f"parts_stored{i}") for i in range(4)]
        v_ps = sem("v_ps")
        v_sb = sem("v_sb")
        v_act_sb = sem("v_act_sb")
        stack_loaded = [sem(f"stack_loaded{i}") for i in range(2)]
        vgrp_ready = sem("vgrp_ready")
        smax_ps = sem("smax_ps")
        smax_read = sem("smax_read")
        mparts_ready = sem("mparts_ready")
        mT_ps = sem("mT_ps")
        mT_ready = sem("mT_ready")
        m_loaded = [sem(f"m_loaded{i}") for i in range(2)]
        score_ps = sem("score_ps")
        prob_ready = sem("prob_ready")
        pv_done = sem("pv_done")
        oT_ready = sem("oT_ready")
        o_ps = sem("o_ps")
        o_normed = sem("o_normed")
        yT_ps = sem("yT_ps")
        yT_ready = sem("yT_ready")
        proj_ps = sem("proj_ps")
        proj_added = sem("proj_added")
        stored = sem("stored")

        xn_tile = lambda t: xn[:, t, 0:P]
        quad = lambda g: slice(4 * g, 4 * g + 4)

        part_stores = lambda i: 1 if i // 2 % 2 else 3

        score_bank = lambda i, final: bank[(4, 5, 0, 1)[i % 4] if final else 4 + i % 2]

        v_bank = lambda i: bank[(2, 3, 6, 7)[i]]
        values_src = lambda i: v_bank(i).rearrange("p (c g h d) -> p g c h d", c=4, g=HEADS // GH, h=GH)
        values_dst = lambda i, g: v_all5[:, i // 2 * GH + g, 4 * (i % 2):4 * (i % 2) + 4, :, 0:HD]

        block = ctx.enter_context(nc.Block())

        @block.sync
        def _(sp):
            for g in range(QUADS):
                sp.dma_start(xres[:, quad(g), :], x_view[:, quad(g), :]).then_inc(x_loaded[g], 16)
            for dst, src in ((gate_sb[:, :], gate_w), (w_sh[:, 0:INNER], sh_gate), (w_sh[:, INNER:2 * INNER], sh_up),
                             (w_sh[:, 2 * INNER:].rearrange("p (c h) -> p c h", c=2), sh_down.rearrange("(c p) h -> p c h", p=P)),
                             (wv_sb[:, :], w_qkv_v), (wut_sb[:, :], w_qkv_ut), (wov_sb[:, :], w_o_v), (wout_sb[:, :], w_o_ut)):
                sp.dma_start(dst, src).then_inc(small_loaded, 16)
            sp.wait_ge(consts_ready, 1)

            def prefill(n):
                sp.dma_start(rows_dram[n].rearrange("(j p) r -> p j r", p=P),
                             empty_row[:, :].unsqueeze(1).broadcast_to([P, SLOT_TILES, ROW])).then_inc(prefilled[n], 16)

            prefill(0)
            w3 = w_exp[:, :].rearrange("p (e w) -> p e w", w=WROW)
            step = EXPERTS // 4
            for e in range(0, EXPERTS, step):
                sp.dma_start(w3[:, e:e + step, 0:INNER], r_gate[e:e + step].rearrange("e h i -> h e i")).then_inc(experts_loaded, 16)
                sp.dma_start(w3[:, e:e + step, INNER:2 * INNER], r_up[e:e + step].rearrange("e h i -> h e i")).then_inc(experts_loaded, 16)
                for c in range(2):
                    sp.dma_start(w3[:, e:e + step, 2 * INNER + c * P:2 * INNER + (c + 1) * P],
                                 r_down[e:e + step, c * P:(c + 1) * P, :].rearrange("e p h -> p e h")).then_inc(experts_loaded, 16)

            def ffn(n):
                sp.wait_ge(scattered, 16 * TILES * (n + 1))

                def load(j, r):
                    at_least(sp, xeT_ps, n * SLOT_TILES + j - 3)
                    at_least(sp, ids_done, n * SLOT_TILES + j - 3)
                    sp.dma_start(xe[r][:, :], rows_dram[n][bass.ds(j * P, P), :]).then_inc(xe_loaded[r], 16)

                for r in range(4):
                    load(r, r)
                with sp.Fori(1, SLOT_TILES // 4) as k:
                    for r in range(4):
                        load(4 * k + r, r)
                for j in range(SLOT_TILES // 4 * 4, SLOT_TILES):
                    load(j, j % 4)
                for i in range(4):
                    sp.wait_ge(y_stored[i], ring_signals(n + 1, i, i))
                y_view = y_dram[n].rearrange("(t p) h -> p t h", p=P)
                for g in range(QUADS):
                    sp.dma_start(y_back[:, quad(g), :], y_view[:, quad(g), :]).then_inc(y_loaded[g], 16)

            def attention():
                def store_parts(i):
                    b, half = i // 4, i % 2
                    sp.wait_ge(part2_sb, i + 1)
                    if i // 2 % 2:
                        sp.dma_start(k_dram[:, b * P:(b + 1) * P, half * QW:(half + 1) * QW].rearrange("c p t -> p c t"),
                                     part_sb[i % 4]).then_inc(parts_stored[i % 4], 16)
                    else:
                        for c in range(3):
                            dst = q_dram[c, b * P // GH:(b + 1) * P // GH, half * GH * QW:(half + 1) * GH * QW]
                            sp.dma_start(dst.rearrange("r (h t) -> r h t", t=QW), part_sb[i % 4][:, c, :])\
                                .then_inc(parts_stored[i % 4], 16)

                def load_stacks(g, r):
                    row = 0
                    for part, n in enumerate(Q_OF_K):
                        rows = slice(row, row + n * HD)
                        row += n * HD
                        q = q_dram[0:n, bass.ds(g * HD, HD), :]
                        k = k_dram[part, bass.ds(g * GH * HD, GH * HD), :].rearrange("(d h) t -> d (h t)", h=GH)
                        sp.dma_start(q_stack[r][rows, :, :, :].rearrange("p a h t -> p (a h t)"), q).then_inc(stack_loaded[r], 16)
                        sp.dma_start(k_stack[r][rows, :, :].rearrange("p h t -> p (h t)"),
                                     k.unsqueeze(0).broadcast_to([n, HD, GH * SEQ])).then_inc(stack_loaded[r], 16)

                def load_m(u):
                    half, r = u[1] % 2, u[1] // 2 % 2
                    sp.wait_ge(mT_ready, u[0] + 1)
                    for c in range(3):
                        dst = q_stack[r][MROW + c:MROW + c + 1, half, :, :].rearrange("o h t -> o (h t)")
                        src = mT[c * MBLOCKS:(c + 1) * MBLOCKS, :]
                        sp.dma_start(dst, src).then_inc(m_loaded[half], 16)

                for i in range(4):
                    store_parts(i)
                sp.wait_ge(stacks_cleared, 1)
                for i in range(4):
                    sp.wait_ge(parts_stored[i], 16 * part_stores(i))
                load_stacks(0, 0)
                load_stacks(1, 1)
                for i in range(4, 8):
                    store_parts(i)
                for i in range(4):
                    sp.wait_ge(parts_stored[i], 32 * part_stores(i))
                load_m((0, 0))
                with sp.Fori(0, GROUPS // 2 - 1) as k:
                    for s in range(4):
                        load_m((4 * k + s + 1, s + 1))
                        if s % 2:
                            sp.wait_ge(pv_done, CHUNKS * (4 * k + s + 1))
                            load_stacks(2 * k + s // 2 + 2, s // 2)
                for s in range(3):
                    load_m((UNITS - 4 + s + 1, s + 1))

            ffn(0)
            prefill(1)
            attention()
            ffn(1)
            for g in range(QUADS):
                sp.wait_ge(out_ready, g + 1)
                sp.dma_start(out_view[:, quad(g), :], xres[:, quad(g), :]).then_inc(stored, 16)
            sp.wait_ge(stored, 16 * QUADS)

        @block.gpsimd
        def _(pool):
            own = Tally(pool_own)
            nc.gpsimd.memset(empty_row[:, 0:P], 0.0)
            nc.gpsimd.memset(empty_row[:, P:ROW].bitcast(I32), NOWHERE).then_inc(consts_ready, 1)
            nc.gpsimd.memset(identf[:, :], 0.0)
            nc.gpsimd.memset(identb[:, :], 0.0)
            nc.gpsimd.memset(before[:, :], 1.0)
            nc.gpsimd.memset(onesb[:, :], 1.0)
            nc.gpsimd.memset(zeros[:, :], 0.0)
            nc.gpsimd.iota(xn[:, :, P:ROW].bitcast(I32), pattern=[[P, TILES], [0, 4]], base=0, channel_multiplier=1)
            nc.gpsimd.iota(slot_tile_i[:, :], pattern=[[0, 1]], base=0, channel_multiplier=1)
            w = own.done(nc.gpsimd.iota(iota_i[:, :], pattern=[[-1, EXPERTS]], base=EXPERTS, channel_multiplier=0))
            pool.wait_ge(pool_own, w)
            nc.gpsimd.affine_select(out=identf[:, :], in_=identf[:, :], compare_op=ALU.not_equal, fill=1.0,
                                    base=0, pattern=[[-1, P]], channel_multiplier=1)
            nc.gpsimd.affine_select(out=identb[:, :], in_=identb[:, :], compare_op=ALU.not_equal, fill=1.0,
                                    base=0, pattern=[[-1, P]], channel_multiplier=1)
            nc.gpsimd.affine_select(out=before[:, :], in_=before[:, :], compare_op=ALU.is_gt, fill=0.0,
                                    base=0, pattern=[[1, P]], channel_multiplier=-1)
            nc.gpsimd.tensor_copy(slot_tile[:, :], slot_tile_i[:, :])
            nc.gpsimd.tensor_copy(rev[:, :], iota_i[:, :]).then_inc(consts_ready, 1)
            for i in range(2):
                nc.gpsimd.memset(q_stack[i][:, :, :, :].bitcast(F32), 0.0)
                nc.gpsimd.memset(k_stack[i][0:MROW, :, :].bitcast(F32), 0.0)
            pool.wait_ge(pool_own, own.done(nc.gpsimd.memset(v_all[:, :, :], 1.0)))
            for i in range(2):
                w = own.done(nc.gpsimd.memset(k_stack[i][MROW:P, :, :], 1.0))
            pool.wait_ge(pool_own, w)
            pool.sem_inc(stacks_cleared, 1)

            def ffn(n):
                pool.wait_ge(prefilled[n], 16)
                for t in range(TILES):
                    if t % 4 == 0:
                        pool.wait_ge(slots_ready, n * QUADS + t // 4 + 1)
                    nc.gpsimd.indirect_dma_start(
                        rows_dram[n], bass.IndirectOffsetOnAxis(slot_i[:, t:t + 1].bitcast(U32), 0),
                        xn[:, t, :], None).then_inc(scattered, 16)

                def store(j, r):
                    pool.wait_ge(y_done, n * SLOT_TILES + j + 1)
                    pool.sem_inc(stores_begun, 1)
                    nc.gpsimd.indirect_dma_start(
                        y_dram[n], bass.IndirectOffsetOnAxis(slot_token[:, r:r + 1].bitcast(U32), 0),
                        yb[r % 4][:, :], None, bounds_check=TOKENS - 1, oob_is_err=False).then_inc(y_stored[r % 4], 16)

                with pool.Fori(0, SLOT_TILES // 8) as k:
                    for r in range(8):
                        store(8 * k + r, r)
                for j in range(LAST_TILES, SLOT_TILES):
                    store(j, j % 8)

            def attention():
                pool.wait_ge(xn_ready, QUADS + 1)
                nc.gpsimd.memset(mpart[:, :, :], 0.0)
                for i in range(2):
                    last = nc.gpsimd.memset(arena2[:, i], 0.0)
                pool.wait_ge(pool_own, own.done(last))

                def values(g, r):
                    src = v_all[:, bass.ds(g, 1), :].rearrange("p o (c h d) -> p (o c) h d", c=CHUNKS, h=GH)
                    nc.gpsimd.tensor_copy(v_grp[r][:, :, :, 0:HD + 1], src).then_inc(vgrp_ready, 1)

                def m_parts(u, half):
                    pool.wait_ge(smax_read, MBLOCKS * (u + 1))
                    at_least(pool, mT_ps, u)
                    m = rowmax[half][:, :]
                    zero = zeros[:, 0:MBLOCKS]
                    pool.wait_ge(pool_own, own.done(nc.gpsimd.tensor_tensor(mpart[:, 0, :], zero, m, ALU.subtract)))
                    pool.wait_ge(pool_own, own.done(nc.gpsimd.tensor_tensor(mrest[:, :], m, mpart[:, 0, :], ALU.add)))
                    pool.wait_ge(pool_own, own.done(nc.gpsimd.tensor_tensor(mpart[:, 1, :], zero, mrest[:, :], ALU.subtract)))
                    pool.wait_ge(pool_own, own.done(nc.gpsimd.tensor_tensor(mrest[:, :], mrest[:, :], mpart[:, 1, :], ALU.add)))
                    nc.gpsimd.tensor_tensor(mpart[:, 2, :], zero, mrest[:, :], ALU.subtract).then_inc(mparts_ready, 1)

                def rest(i):
                    pool.wait_ge(part0_sb, i + 1)
                    nc.gpsimd.tensor_tensor(rest_sb[i % 2], rest_sb[i % 2], part_sb[i % 4][:, 0, :],
                                            ALU.subtract).then_inc(rest_pool_ready, 1)

                def part2(i):
                    pool.wait_ge(part1_sb, i + 1)
                    nc.gpsimd.tensor_tensor(part_sb[i % 4][:, 2, :], rest_sb[i % 2], part_sb[i % 4][:, 1, :],
                                            ALU.subtract).then_inc(part2_sb, 1)

                for i in range(4):
                    part2(i)
                pool.wait_ge(v_sb, 2)
                values(0, 0)
                values(1, 1)
                for i in (4, 6):
                    rest(i)
                    rest(i + 1)
                    part2(i)
                    part2(i + 1)
                m_parts(0, 0)
                pool.wait_ge(v_act_sb, 2)
                per = 16
                start = own.n
                with pool.Fori(0, GROUPS // 2 - 1) as k:
                    own.base, own.n = start + k * per, 0
                    for s in range(4):
                        m_parts(4 * k + s + 1, (s + 1) % 2)
                        if s % 2:
                            pool.wait_ge(pv_done, 8 * (4 * k + s + 1))
                            values(2 * k + s // 2 + 2, s // 2)
                    assert own.n == per
                own.base, own.n = 0, start + per * (GROUPS // 2 - 1)
                for s in range(3):
                    m_parts(UNITS - 4 + s + 1, (s + 1) % 2)

            ffn(0)
            attention()
            ffn(1)

        @block.scalar
        def _(act):
            def xnT_out(use, g, b):
                act.wait_ge(xnT_ps, use * QUADS + g + 1)
                nc.scalar.activation(xnT[:, g * BANK:(g + 1) * BANK], b, ACT.Copy).then_inc(xnT_ready, 1)

            def transposed(use, first=0, last=QUADS):
                act.wait_ge(rstd_ready, (1, 2 + first // 2, 4)[use])
                for g in range(first, last + 1):
                    if g < last:
                        t = 4 * g + 3
                        nc.scalar.activation(xn_tile(t), xres[:, t, :], ACT.Identity, scale=rstd[:, t:t + 1],
                                             bias=shift[:, t:t + 1]).then_inc(xn_act_ready, 1)
                    if g > first:
                        xnT_out(use, g - 1, bank[(g - 1) % 2])

            def ffn(n):
                transposed(2 * n, first=n * (QUADS - 1))
                act.wait_ge(top_ready, n + 1)
                nc.scalar.activation(escore[:, :], top[:, :], ACT.Exp, scale=-1.0).then_inc(escore_ready, 1)
                for i in range(2 * QUADS):
                    act.wait_ge(shg_ps, 8 * n + i + 1)
                    at_least(act, shh_sb, 8 * n + i - 1)
                    nc.scalar.activation(silu_sb[i % 2], bank[5 * (i % 2)][:, :], ACT.Silu).then_inc(shsilu_sb, 1)

                base = n * SLOT_TILES

                def x_out(j, r):
                    act.wait_ge(xeT_ps, base + j + 1)
                    at_least(act, gu_ps, base + j - 1)
                    nc.scalar.activation(xeT[r % 2][:, :], bank[5 + r % 2][:, 0:P], ACT.Copy).then_inc(xeT_sb, 1)

                def silu(j, r):
                    act.wait_ge(gu_ps, base + j + 1)
                    at_least(act, h_done, base + j - 1)
                    nc.scalar.activation(silu_sb[r % 2][:, 0:INNER], bank[r % 2][:, 0:INNER], ACT.Silu).then_inc(silu_done, 1)

                def y_out(j, r):
                    act.wait_ge(y_ps, base + j + 1)
                    at_least(act, y_stored[r % 4], ring_signals(n, j, r))
                    nc.scalar.activation(yb[r % 4][:, :], bank[(4, 7)[r % 2]][:, 0:P], ACT.Copy).then_inc(y_done, 1)

                act.wait_ge(shh_sb, 8 * (n + 1))
                x_out(0, 0)

                def turn(j, r):
                    if not isinstance(j, int) or j + 1 < SLOT_TILES:
                        x_out(j + 1, r + 1)
                    silu(j, r)
                    if not isinstance(j, int) or j >= 3:
                        y_out(j - 3, r + 5)

                for j in range(8):
                    turn(j, j)
                with act.Fori(1, SLOT_TILES // 8) as k:
                    for r in range(8):
                        turn(8 * k + r, r)
                for j in range(LAST_TILES, SLOT_TILES):
                    turn(j, j)
                for j in range(SLOT_TILES - 3, SLOT_TILES):
                    y_out(j, j)

            def attention():
                act.wait_ge(weights_ps, 1)
                for part in range(2):
                    nc.scalar.activation(w_qkv[:, part * P:(part + 1) * P].rearrange("p (g d h) -> p g h d", g=HEADS // GH, h=GH),
                                         bank[7][:, part * P:(part + 1) * P].rearrange("p (g h d) -> p g h d", h=GH, d=HD), ACT.Copy)
                nc.scalar.activation(w_qkv[:, 2 * P:3 * P], bank[7][:, 2 * P:3 * P], ACT.Copy)
                nc.scalar.activation(w_out[:, :], bank[7][:, 3 * P:4 * P], ACT.Copy).then_inc(weights_sb, 1)
                transposed(1, 0, 2)

                def part0(i):
                    act.wait_ge(qk_ps, i + 1)
                    if i >= 4:
                        act.wait_ge(parts_stored[i % 4], 16 * part_stores(i))
                        act.wait_ge(part2_sb, i - 1)
                        nc.scalar.activation(rest_sb[i % 2], bank[4 + i % 4][:, :], ACT.Copy)
                    nc.scalar.activation(part_sb[i % 4][:, 0, :], bank[4 + i % 4][:, :], ACT.Copy).then_inc(part0_sb, 1)

                def part1(i):
                    if i < 4:
                        act.wait_ge(rest_ready, i + 1)
                    else:
                        act.wait_ge(rest_pool_ready, i - 3)
                    nc.scalar.activation(part_sb[i % 4][:, 1, :], rest_sb[i % 2], ACT.Copy).then_inc(part1_sb, 1)

                part0(0)
                for i in range(1, 4):
                    part0(i)
                    part1(i - 1)
                part1(3)
                transposed(1, 2, 4)
                for i in (4, 6):
                    part0(i)
                    part0(i + 1)
                    part1(i)
                    part1(i + 1)
                act.wait_ge(stacks_cleared, 1)
                for i in range(2, 4):
                    act.wait_ge(v_ps, i + 1)
                    src = values_src(i)
                    for g in range(HEADS // GH):
                        ins = nc.scalar.activation(values_dst(i, g), src[:, g], ACT.Copy)
                    ins.then_inc(v_act_sb, 1)

                def m_out(u):
                    act.wait_ge(mT_ps, u + 1)
                    if not (isinstance(u, int) and u == 0):
                        act.wait_ge(score_ps, STEPS * (u - 1) + 1)
                    nc.scalar.activation(mT[:, :], bank[7][0:3 * MBLOCKS, 0:P // 2].bitcast(BF16), ACT.Copy).then_inc(mT_ready, 1)

                def yT_out(g):
                    act.wait_ge(yT_ps, g + 1)
                    nc.scalar.activation(xnT[:, g * BANK:(g + 1) * BANK], bank[3], ACT.Copy).then_inc(yT_ready, 1)

                def unit(u, s, left=9):
                    for c in range(CHUNKS):
                        for h in range(GH):
                            i = c * GH + h
                            act.wait_ge(score_ps, STEPS * u + i + 1)
                            at_least(act, pv_done, CHUNKS * u + c - 1)
                            nc.scalar.activation(prob[i % 8], score_bank(i, left == 1)[:, :], ACT.Exp, scale=SCALE).then_inc(prob_ready, 1)
                            if i == 3 and not (isinstance(u, int) and u == 0):
                                sums_out(u - 1)
                            if i == 26 and left > 1:
                                m_out(u + 1)
                            if left == 2 and i == 28:
                                yT_out(0)
                            if left == 1 and i in (0, 16):
                                yT_out({0: 1, 16: 2}[i])
                            if left == 1 and i in (24, 28):
                                xnT_out(2, {24: 0, 28: 1}[i], bank[3])

                def sums_out(u):
                    act.wait_ge(pv_done, CHUNKS * (u + 1))
                    at_least(act, o_ps, u)
                    nc.scalar.activation(oT[:, :], bank[6], ACT.Copy).then_inc(oT_ready, 1)

                m_out(0)
                nc.scalar.activation(escore[:, :], top[:, :], ACT.Exp)
                for i in range(4):
                    act.wait_ge(parts_stored[i], 32 * part_stores(i))
                for s in range(4):
                    unit(s, s)
                with act.Fori(1, GROUPS // 2 - 1) as k:
                    for s in range(4):
                        unit(4 * k + s, s)
                for s in range(4):
                    unit(UNITS - 4 + s, s, left=4 - s)
                xnT_out(2, 2, bank[3])
                sums_out(UNITS - 1)
                yT_out(QUADS - 1)

            ffn(0)
            attention()
            ffn(1)

        @block.vector
        def _(dve):
            own = Tally(dve_own)

            def after(ins):
                dve.wait_ge(dve_own, own.done(ins))

            def add_projection(g):
                rows = xres[:, quad(g), :]
                dve.wait_ge(proj_ps, g + 1)
                return nc.vector.tensor_tensor(rows, rows, bank[7].rearrange("p (t h) -> p t h", h=P), ALU.add)\
                    .then_inc(proj_added, 1)

            def statistics(first, last):
                for t in range(4 * first, 4 * last):
                    ins = nc.vector.bn_stats(stats[:, t, :], xres[:, t, :])
                after(ins)
                for t in range(4 * first, 4 * last):
                    ins = nc.vector.bn_aggr(mv[:, t, :], stats[:, t, :])
                after(ins)

            def inverse_std(first, last):
                tiles = slice(4 * first, 4 * last)
                v, r, h = var[:, tiles], rstd[:, tiles], newton[:, tiles]
                after(nc.vector.tensor_scalar(v, mv[:, tiles, 1], EPS, None, ALU.add))
                after(nc.vector.tensor_scalar(seed[:, tiles], v.bitcast(I32), 1, None, ALU.logical_shift_right))
                after(nc.vector.tensor_scalar(r.bitcast(I32), seed[:, tiles], -1.0, float(RSQRT_SEED), ALU.mult, ALU.add))
                for _ in range(NEWTON_STEPS):
                    after(nc.vector.scalar_tensor_tensor(out=h, in0=r, scalar=-0.5, in1=r, op0=ALU.mult, op1=ALU.mult))
                    after(nc.vector.tensor_tensor(h, h, v, ALU.mult))
                    after(nc.vector.scalar_tensor_tensor(out=r, in0=h, scalar=1.5, in1=r, op0=ALU.add, op1=ALU.mult))

            def rows(g, n):
                for t in range(4 * g, 4 * g + n):
                    ins = nc.vector.tensor_scalar(xn_tile(t), xres[:, t, :], mv[:, t, 0:1], rstd[:, t:t + 1],
                                                  ALU.subtract, ALU.mult)
                ins.then_inc(xn_ready, 1)

            def normalize(use, first=0, last=QUADS):
                if use == 2:
                    first = QUADS - 1
                    add_projection(first)
                    dve.wait_ge(proj_added, QUADS)
                    statistics(first, QUADS)
                elif use:
                    for g in range(first, last):
                        x = xres[:, quad(g), :]
                        dve.wait_ge(y_loaded[g], 16 * ((use + 1) // 2))
                        ins = nc.vector.scalar_tensor_tensor(out=x, in0=y_back[:, quad(g), :], scalar=0.5, in1=x,
                                                             op0=ALU.mult, op1=ALU.add)
                        if use == 3:
                            ins.then_inc(out_ready, 1)
                    if use == 3:
                        return
                    after(ins)
                    statistics(first, last)
                else:
                    for g in range(QUADS):
                        dve.wait_ge(x_loaded[g], 16)
                        statistics(g, g + 1)
                inverse_std(first, last)
                tiles = slice(4 * first, 4 * last)
                nc.vector.scalar_tensor_tensor(out=shift[:, tiles], in0=mv[:, tiles, 0], scalar=-1.0, in1=rstd[:, tiles],
                                               op0=ALU.mult, op1=ALU.mult).then_inc(rstd_ready, 1)
                for g in range(first, last):
                    rows(g, 3)

            def ffn(n):
                dve.wait_ge(consts_ready, 2)
                normalize(2 * n)
                logits = bank[2].rearrange("p (t e) -> p t e", e=EXPERTS)
                wide = lambda a: a.unsqueeze(2).broadcast_to([P, TILES, EXPERTS])
                rev3 = rev[:, :].unsqueeze(1).broadcast_to([P, TILES, EXPERTS])
                dve.wait_ge(logits_ready, n + 1)
                ins = nc.vector.tensor_reduce(top[:, :], logits, AX_X, ALU.max)
                ins.then_inc(top_ready, 1)
                dve.wait_ge(top_ready, n + 1)
                after(nc.vector.tensor_tensor(hit, logits, wide(top[:, :]), ALU.is_equal))
                after(nc.vector.tensor_tensor(cand, hit, rev3, ALU.mult))
                after(nc.vector.tensor_reduce(rtop[:, :], cand, AX_X, ALU.max))
                nc.vector.tensor_tensor(onehot3, rev3, wide(rtop[:, :]), ALU.is_equal).then_inc(onehot_ready, 1)

                def sh_product(i):
                    dve.wait_ge(shsilu_sb, 8 * n + i + 1)
                    at_least(dve, shy_ps, 4 * n + i // 2 - 1)
                    nc.vector.tensor_tensor(h_sh[i // 2 % 2][i % 2], bank[1 + 5 * (i % 2)][:, :], silu_sb[i % 2],
                                            ALU.mult).then_inc(shh_sb, 1)

                def sh_add(q):
                    dve.wait_ge(shy_ps, 4 * n + q + 1)
                    nc.vector.scalar_tensor_tensor(out=xres[:, quad(q), :], in0=bank[7].rearrange("p (t h) -> p t h", h=P),
                                                   scalar=0.5, in1=xres[:, quad(q), :], op0=ALU.mult, op1=ALU.add)\
                        .then_inc(shy_added, 1)

                dve.wait_ge(escore_ready, n + 1)
                after(nc.vector.tensor_scalar(escore[:, :], escore[:, :], 1.0, None, ALU.add))
                after(nc.vector.reciprocal(score[:, :], escore[:, :]))
                sh_product(0)
                after(nc.vector.tensor_tensor(xn[:, :, 0:P], xn[:, :, 0:P], score[:, :].unsqueeze(2).broadcast_to([P, TILES, P]), ALU.mult))
                dve.wait_ge(ranks_ready, n + 1)
                count = bank[4][:, 0:EXPERTS]
                after(nc.vector.tensor_scalar(count_i[:, :], count, float(P - 1), None, ALU.add))
                after(nc.vector.tensor_scalar(count_i[:, :], count_i[:, :], 7, 7, ALU.logical_shift_right, ALU.logical_shift_left))
                after(nc.vector.tensor_copy(slots_of[:, :], count_i[:, :]))
                after(nc.vector.tensor_tensor_scan(slots_to[:, :], slots_of[:, :], zeros[:, :], 0.0, ALU.add, ALU.add))
                after(nc.vector.tensor_tensor(base_e[:, :], slots_to[:, :], slots_of[:, :], ALU.subtract))
                ranks = bank[3].rearrange("p (t e) -> p t e", e=EXPERTS)
                for g in range(QUADS):
                    q = quad(g)
                    after(nc.vector.tensor_tensor(place[:, q], ranks[:, q], base_e[:, :].unsqueeze(1).broadcast_to([P, 4, EXPERTS]),
                                                  ALU.add))
                    after(nc.vector.tensor_tensor(place[:, q], place[:, q], onehot3[:, q], ALU.mult))
                    after(nc.vector.tensor_reduce(slot_f[:, q], place[:, q], AX_X, ALU.add))
                    nc.vector.tensor_copy(slot_i[:, q], slot_f[:, q]).then_inc(slots_ready, 1)
                    if g < 3:
                        sh_product(g + 1)
                after(nc.vector.tensor_scalar(below[:, :], slots_to[:, :], 1.0 / P, None, ALU.mult))
                after(nc.vector.tensor_scalar(below[:, :], below[:, :], slot_tile[:, 0:1], None, ALU.is_le))
                after(nc.vector.tensor_reduce(eid[:, :], below[:, :], AX_X, ALU.add))
                nc.vector.tensor_scalar(eid[:, :], eid[:, :], float(EXPERTS - 1), float(WROW), ALU.min, ALU.mult).then_inc(eid_ready, 1)
                sh_add(0)
                sh_product(4)
                dve.wait_ge(eid_row, n + 1)
                nc.vector.tensor_copy(woff[:, :], bank[4][0:1, P:2 * P]).then_inc(woff_ready, 1)
                sh_product(5)
                sh_add(1)
                sh_product(6)
                sh_product(7)
                sh_add(2)
                sh_add(3)

                base = n * SLOT_TILES

                def hT_out(j, r):
                    dve.wait_ge(hT_ps, base + j + 1)
                    at_least(dve, y_ps, base + j - 1)
                    nc.vector.tensor_copy(hT_sb[r % 2], bank[2 + r % 2][:, 0:INNER]).then_inc(hT_done, 1)

                def product(j, r):
                    dve.wait_ge(silu_done, base + j + 1)
                    at_least(dve, hT_ps, base + j - 1)
                    nc.vector.tensor_tensor(h_sb[r % 2], bank[r % 2][:, INNER:2 * INNER], silu_sb[r % 2][:, 0:INNER],
                                            ALU.mult).then_inc(h_done, 1)

                def ids(j, r):
                    dve.wait_ge(xe_loaded[r % 4], ring_signals(n, j, r) + 16)
                    at_least(dve, y_stored[r % 4], ring_signals(n, j, r) - 16)
                    nc.vector.tensor_copy(slot_token[:, r % 8:r % 8 + 1], xe[r % 4][:, P:P + 1].bitcast(I32)).then_inc(ids_done, 1)

                def turn(j, r):
                    product(j, r)
                    if not isinstance(j, int) or j >= 2:
                        hT_out(j - 2, r)
                    if not isinstance(j, int) or j + 1 < SLOT_TILES:
                        ids(j + 1, r + 1)

                ids(0, 0)
                for j in range(8):
                    turn(j, j)
                with dve.Fori(1, SLOT_TILES // 8) as k:
                    for r in range(8):
                        turn(8 * k + r, r)
                for j in range(LAST_TILES, SLOT_TILES):
                    turn(j, j)
                for j in range(SLOT_TILES - 2, SLOT_TILES):
                    hT_out(j, j)

            def attention():
                normalize(1, 0, 2)
                for i in range(4):
                    dve.wait_ge(part0_sb, i + 1)
                    at_least(dve, part2_sb, i - 1)
                    nc.vector.tensor_tensor(rest_sb[i % 2], bank[4 + i % 4][:, :], part_sb[i % 4][:, 0, :],
                                            ALU.subtract).then_inc(rest_ready, 1)
                dve.wait_ge(stacks_cleared, 1)
                for i in range(2):
                    dve.wait_ge(v_ps, i + 1)
                    src = values_src(i)
                    for g in range(HEADS // GH):
                        ins = nc.vector.tensor_copy(values_dst(i, g), src[:, g])
                    ins.then_inc(v_sb, 1)
                normalize(1, 2, 4)

                def row_max(u, m):
                    i = MBLOCKS * u[0] + m
                    dve.wait_ge(smax_ps, i + 1)
                    at_least(dve, mparts_ready, u[0] - 1)
                    nc.vector.tensor_reduce(rowmax[u[1] % 2][:, m:m + 1], pair[m % 2][:, :], AX_X, ALU.max).then_inc(smax_read, 1)

                def store_norm(u, b, g, half):
                    dve.wait_ge(o_ps, u + 1)
                    o = bank[7].rearrange("p (t h d) -> p t h d", t=4, h=GH)
                    after(nc.vector.reciprocal(rden[:, :, :], o[:, :, :, HD]))
                    t0 = 8 * b + 4 * half
                    for t in range(4):
                        dst = xn[:, bass.ds(t0 + t, 1), bass.ds(g * GH * HD, GH * HD)].rearrange("p o (h d) -> p (o h) d", d=HD)
                        ins = nc.vector.tensor_tensor(dst, o[:, t, :, 0:HD],
                                                      rden[:, t, :].unsqueeze(2).broadcast_to([P, GH, HD]), ALU.mult)
                    ins.then_inc(o_normed, 1)

                def unit(u, s, b, g, first=False, left=9):
                    for c, blocks in enumerate(MAXIMA):
                        for ahead, m in blocks:
                            if ahead < left:
                                row_max((u + ahead, s + ahead), m)
                        if c == 2 and not first and left > 1:
                            store_norm(u - 1, b, g, (s + 1) % 2)

                def residual(g):
                    add_projection(g)
                    dve.wait_ge(proj_added, g + 1)
                    statistics(g, g + 1)

                for m in range(MBLOCKS):
                    row_max((0, 0), m)
                for m in range(AHEAD):
                    row_max((1, 1), m)
                unit(0, 0, 0, 0, first=True)
                for s in range(1, 4):
                    unit(s, s, 0, (s - 1) // 2)
                start = own.n
                per = 4
                with dve.Fori(1, GROUPS // 2 - 1) as k:
                    own.base, own.n = start + (k - 1) * per, 0
                    unit(4 * k, 0, 0, 2 * k - 1)
                    for s in range(1, 4):
                        unit(4 * k + s, s, k - 1, 4 - 2 * k + (s - 1) // 2)
                    assert own.n == per
                own.base, own.n = 0, start + per * (GROUPS // 2 - 2)
                unit(UNITS - 4, 0, 1, 1)
                unit(UNITS - 3, 1, 1, 2)
                unit(UNITS - 2, 2, 1, 2, left=2)
                unit(UNITS - 1, 3, 1, 3, left=1)
                residual(0)
                residual(1)
                inverse_std(0, 2)
                store_norm(UNITS - 2, 1, 3, 0)
                rows(0, 4)
                rows(1, 4)
                residual(2)
                inverse_std(2, 3)
                rows(2, 4)
                store_norm(UNITS - 1, 1, 3, 1)

            ffn(0)
            attention()
            ffn(1)
            normalize(3)

        @block.tensor
        def _(pe):
            pe.wait_ge(consts_ready, 2)

            def transpose_rows(use, g, b):
                pe.wait_ge(xn_ready, use * QUADS + g + 1)
                if use < 2:
                    pe.wait_ge(xn_act_ready, use * QUADS + g + 1)
                elif g == QUADS - 1:
                    pe.wait_ge(xn_act_ready, 2 * QUADS + 1)
                for t in range(4):
                    ins = nc.tensor.transpose(b[:, t * P:(t + 1) * P], xn_tile(4 * g + t), identf[:, :])
                ins.then_inc(xnT_ps, 1)

            def logits(n, g):
                if n == 0 and g == 0:
                    pe.wait_ge(small_loaded, 16 * 8)
                pe.wait_ge(xnT_ready, 2 * n * QUADS + g + 1)
                for t in range(4 * g, 4 * g + 4):
                    ins = nc.tensor.matmul(bank[2][:, t * EXPERTS:(t + 1) * EXPERTS], xnT[:, t * P:(t + 1) * P], gate_sb[:, :],
                                           start=True, stop=True)
                if g == QUADS - 1:
                    ins.then_inc(logits_ready, 1)

            def ffn(n):
                if n == 0:
                    for g in range(QUADS):
                        at_least(pe, xnT_ready, g - 1)
                        transpose_rows(0, g, bank[g % 2])
                        if g:
                            logits(0, g - 1)
                else:
                    transpose_rows(2, QUADS - 1, bank[1])
                logits(n, QUADS - 1)

                def sh_up(i):
                    q, c = i // 2, i % 2
                    at_least(pe, shh_sb, 8 * n + i - 1)
                    for part, b in ((0, bank[5 * c]), (INNER, bank[1 + 5 * c])):
                        ins = nc.tensor.matmul(b[:, :], w_sh[:, part + c * P:part + (c + 1) * P], xnT[:, q * BANK:(q + 1) * BANK],
                                               start=True, stop=True)
                    ins.then_inc(shg_ps, 1)

                def sh_down(q):
                    pe.wait_ge(shh_sb, 8 * n + 2 * q + 2)
                    at_least(pe, shy_added, 4 * n + q)
                    for t in range(4):
                        for c in range(2):
                            ins = nc.tensor.matmul(bank[7][:, t * P:(t + 1) * P], h_sh[q % 2][c][:, t * P:(t + 1) * P],
                                                   w_sh[:, 2 * INNER + c * P:2 * INNER + (c + 1) * P], start=(c == 0), stop=(c == 1))
                    ins.then_inc(shy_ps, 1)

                sh_up(0)
                pe.wait_ge(onehot_ready, n + 1)
                for t in range(TILES):
                    nc.tensor.matmul(bank[4][:, 0:EXPERTS], onesb[:, :], onehot[:, t * EXPERTS:(t + 1) * EXPERTS],
                                     start=(t == 0), stop=(t == TILES - 1))
                nc.tensor.matmul(bank[3], before[:, :], onehot, start=True, stop=False)
                for d in range(1, TILES):
                    ins = nc.tensor.matmul(bank[3][:, d * EXPERTS:], onesb[:, :], onehot[:, 0:(TILES - d) * EXPERTS],
                                           start=False, stop=(d == TILES - 1))
                ins.then_inc(ranks_ready, 1)
                sh_up(1)
                sh_up(2)
                sh_up(3)
                sh_down(0)
                pe.wait_ge(eid_ready, n + 1)
                nc.tensor.matmul(bank[4][0:1, P:2 * P], eid[:, :], identf[:, :], start=True, stop=True).then_inc(eid_row, 1)
                sh_up(4)
                sh_up(5)
                sh_down(1)
                sh_up(6)
                sh_up(7)
                sh_down(2)
                sh_down(3)

                base = n * SLOT_TILES

                def x_transpose(j, r):
                    pe.wait_ge(xe_loaded[r % 4], ring_signals(n, j, r) + 16)
                    at_least(pe, xeT_sb, base + j - 1)
                    nc.tensor.transpose(bank[5 + r % 2][:, 0:P], xe[r % 4][:, 0:P], identf[:, :]).then_inc(xeT_ps, 1)

                def weights_of(j, count):
                    _, starts = nc.values_load_multi_w_load_instructions(
                        woff[0:1, bass.ds(j, count)], engines=(mybir.EngineType.PE,), min_val=0, max_val=(EXPERTS - 1) * WROW,
                        skip_runtime_bounds_check_because="VectorE takes the minimum of the expert's number and the last one's")
                    return starts

                def gate_up(j, r, e):
                    pe.wait_ge(xeT_sb, base + j + 1)
                    at_least(pe, h_done, base + j - 1)
                    nc.tensor.matmul(bank[r % 2][:, :], xeT[r % 2][:, :], w_exp[:, bass.ds(e, 2 * INNER)],
                                     start=True, stop=True).then_inc(gu_ps, 1)

                def h_transpose(j, r):
                    pe.wait_ge(h_done, base + j + 1)
                    at_least(pe, hT_done, base + j - 1)
                    for c in range(2):
                        ins = nc.tensor.transpose(bank[2 + r % 2][:, c * P:(c + 1) * P], h_sb[r % 2][:, c * P:(c + 1) * P], identf[:, :])
                    ins.then_inc(hT_ps, 1)

                def down(j, r, e):
                    pe.wait_ge(hT_done, base + j + 1)
                    at_least(pe, y_done, base + j - 1)
                    for c in range(2):
                        ins = nc.tensor.matmul(bank[(4, 7)[r % 2]][:, 0:P], hT_sb[r % 2][:, c * P:(c + 1) * P],
                                               w_exp[:, bass.ds(e + 2 * INNER + c * P, P)], start=(c == 0), stop=(c == 1))
                    ins.then_inc(y_ps, 1)

                pe.wait_ge(woff_ready, n + 1)
                pe.wait_ge(experts_loaded, 16 * 16)
                pe.wait_ge(shy_added, 4 * (n + 1))

                def turn(j, r, e_down, e_next):
                    if e_down is not None or j == 2:
                        h_transpose(j - 2, (r - 2) % 8)
                    if e_down is not None:
                        down(j - 3, (r - 3) % 8, e_down)
                    if not isinstance(j, int) or j + 2 < SLOT_TILES:
                        x_transpose(j + 2, (r + 2) % 8)
                    gate_up(j + 1, (r + 1) % 8, e_next)

                e = weights_of(0, 8)
                x_transpose(0, 0)
                x_transpose(1, 1)
                gate_up(0, 0, e[0])
                for j in range(7):
                    turn(j, j, e[j - 3] if j >= 3 else None, e[j + 1])
                with pe.Fori(1, SLOT_TILES // 8) as k:
                    e = weights_of(8 * k - 4, 12)
                    for i in range(8):
                        turn(8 * k + i - 1, i - 1, e[i], e[i + 4])
                e = weights_of(LAST_TILES - 4, SLOT_TILES - LAST_TILES + 4)
                for i in range(SLOT_TILES - LAST_TILES):
                    turn(LAST_TILES + i - 1, i - 1, e[i], e[i + 4])
                for j in range(SLOT_TILES - 4, SLOT_TILES):
                    if j + 1 < SLOT_TILES:
                        h_transpose(j + 1, j + 1)
                    down(j, j, e[j - LAST_TILES + 4])

            def attention():
                pe.wait_ge(y_done, SLOT_TILES)
                nc.tensor.matmul(bank[7][:, 0:3 * P], wv_sb[:, :], wut_sb[:, :], start=True, stop=True)
                nc.tensor.matmul(bank[7][:, 3 * P:4 * P], wov_sb[:, :], wout_sb[:, :], start=True, stop=True).then_inc(weights_ps, 1)

                def sequence_rows(b):
                    for g in (2 * b, 2 * b + 1):
                        at_least(pe, xnT_ready, QUADS + g - 1)
                        transpose_rows(1, g, bank[g % 2])

                def project_qk(i):
                    b, qk, half = i // 4, i // 2 % 2, i % 2
                    pe.wait_ge(xnT_ready, QUADS + 2 * b + half + 1)
                    at_least(pe, rest_ready, i - 3)
                    nc.tensor.matmul(bank[4 + i % 4][:, :], w_qkv[:, qk * P:(qk + 1) * P],
                                     xnT[:, (2 * b + half) * BANK:(2 * b + half + 1) * BANK], start=True, stop=True).then_inc(qk_ps, 1)

                def project_v(i):
                    for c in range(4):
                        t = 4 * i + c
                        ins = nc.tensor.matmul(v_bank(i)[:, c * P:(c + 1) * P], xnT[:, t * P:(t + 1) * P],
                                               w_qkv[:, 2 * P:3 * P], start=True, stop=True)
                    ins.then_inc(v_ps, 1)

                sequence_rows(0)
                pe.wait_ge(weights_sb, 1)
                for i in range(4):
                    project_qk(i)
                project_v(0)
                project_v(1)
                sequence_rows(1)
                for i in range(4, 8):
                    project_qk(i)
                pe.wait_ge(v_sb, 2)

                def max_scores(u, m, part):
                    h, t, i = m // 4, m % 4, MBLOCKS * u[0] + m
                    r, half = u[1] // 2 % 2, u[1] % 2
                    if part == 0:
                        at_least(pe, smax_read, i - 1)
                    ins = nc.tensor.matmul(pair[m % 2][:, part * BANK:(part + 1) * BANK], q_stack[r][0:MROW, half, h, t * P:(t + 1) * P],
                                           k_stack[r][0:MROW, h, part * BANK:(part + 1) * BANK], start=True, stop=True)
                    if part == 1:
                        ins.then_inc(smax_ps, 1)

                def scores(u, s, i, final):
                    c, h, r, half = i // GH, i % GH, s // 2 % 2, s % 2
                    at_least(pe, prob_ready, STEPS * u + i - (3 if final and i >= 2 else 1))
                    nc.tensor.matmul(score_bank(i, final)[:, :], k_stack[r][:, h, c * P:(c + 1) * P],
                                     q_stack[r][:, half, h, :], start=True, stop=True).then_inc(score_ps, 1)

                def weigh(u, s, c):
                    pe.wait_ge(prob_ready, STEPS * u + GH * (c + 1))
                    if c == 0:
                        at_least(pe, oT_ready, u)
                    for h in range(GH):
                        ins = nc.tensor.matmul(bank[6][32 * h:32 * (h + 1), :], v_grp[s // 2 % 2][:, c, h, :], prob[(c * GH + h) % 8],
                                               start=(c == 0), stop=(c == CHUNKS - 1))
                    ins.then_inc(pv_done, 1)

                def o_transpose(u):
                    pe.wait_ge(oT_ready, u + 1)
                    at_least(pe, o_normed, u)
                    pe.wait_ge(mT_ready, UNITS if isinstance(u, int) and u + 2 > UNITS else u + 2)
                    if isinstance(u, int) and u >= UNITS - 2:
                        pe.wait_ge(proj_added, u - UNITS + 4)
                    for t in range(4):
                        ins = nc.tensor.transpose(bank[7][:, t * P:(t + 1) * P], oT[:, t * P:(t + 1) * P], identf[:, :])
                    ins.then_inc(o_ps, 1)

                def m_transpose(u):
                    pe.wait_ge(mparts_ready, u + 1)
                    at_least(pe, o_normed, u - 1)
                    nc.tensor.transpose(bank[7][:, 0:P // 2].bitcast(BF16),
                                        mpart[:, :, :].rearrange("p c m -> p (c m)"), identb[:, :]).then_inc(mT_ps, 1)

                def out_transpose(g):
                    if g >= 2:
                        pe.wait_ge(o_normed, UNITS - QUADS + g + 1)
                    pe.wait_ge(smax_read, UNITS * MBLOCKS)
                    at_least(pe, yT_ready, g)
                    if g == QUADS - 1:
                        pe.wait_ge(xnT_ready, 2 * QUADS + g)
                    for t in range(4):
                        ins = nc.tensor.transpose(bank[3][:, t * P:(t + 1) * P], xn_tile(4 * g + t), identf[:, :])
                    ins.then_inc(yT_ps, 1)

                def project_out(g):
                    pe.wait_ge(yT_ready, g + 1)
                    pe.wait_ge(mT_ready, UNITS)
                    pe.wait_ge(o_normed, UNITS - QUADS + max(g + 1, 2))
                    at_least(pe, proj_added, g)
                    for t in range(4):
                        at = (4 * g + t) * P
                        ins = nc.tensor.matmul(bank[7][:, t * P:(t + 1) * P], xnT[:, at:at + P], w_out[:, :], start=True, stop=True)
                    ins.then_inc(proj_ps, 1)

                def next_norm(g):
                    at_least(pe, yT_ready, QUADS - 1)
                    pe.wait_ge(xnT_ready, 2 * QUADS + g)
                    transpose_rows(2, g, bank[3])

                beside = {(2, 6): [(out_transpose, 0)], (2, 7): [(project_out, 0), (out_transpose, 1)],
                          (1, 0): [(project_out, 1)], (1, 3): [(out_transpose, 2)], (1, 4): [(project_out, 2)],
                          (1, 5): [(next_norm, 0)], (1, 6): [(next_norm, 1)], (1, 7): [(next_norm, 2)]}

                def unit(u, s, quarter, first=False, left=9):
                    if s % 2 == 0:
                        pe.wait_ge(vgrp_ready, 2 * quarter + s // 2 + 1)
                    pe.wait_ge(m_loaded[s % 2], 16 * 3 * (2 * quarter + s // 2 + 1))

                    def values_before(c):
                        if c:
                            weigh(u, s, c - 1)
                        elif not first:
                            weigh(u - 1, s - 1 + 4, CHUNKS - 1)

                    next_group = s % 2 == 0
                    for c, blocks in enumerate(MAXIMA):
                        blocks = [b for b in blocks if b[0] < left]
                        scores(u, s, GH * c, left == 1)
                        scores(u, s, GH * c + 1, left == 1)
                        for ahead, m in blocks:
                            if ahead == 2 and next_group:
                                pe.wait_ge(stack_loaded[(s // 2 + 1) % 2], 16 * STACK_LOADS * (quarter + (s + 2) // 4 + 1))
                                next_group = False
                            max_scores((u + ahead, s + ahead), m, 0)
                            max_scores((u + ahead, s + ahead), m, 1)
                        if c == 6 and left > 1:
                            m_transpose(u + 1)
                        if not blocks:
                            values_before(c)
                        scores(u, s, GH * c + 2, left == 1)
                        scores(u, s, GH * c + 3, left == 1)
                        if blocks:
                            values_before(c)
                        if c == 2 and not first:
                            o_transpose(u - 1)
                        for work, quad_done in beside.get((left, c), ()):
                            work(quad_done)

                pe.wait_ge(stack_loaded[0], 16 * STACK_LOADS)
                for m in range(MBLOCKS):
                    for part in range(2):
                        max_scores((0, 0), m, part)
                    if m in (8, 9):
                        pe.wait_ge(part0_sb, m - 1)
                        project_v(m - 6)
                pe.wait_ge(v_act_sb, 2)
                for m in range(AHEAD):
                    for part in range(2):
                        max_scores((1, 1), m, part)
                    if m == 2:
                        m_transpose(0)
                for s in range(4):
                    unit(s, s, 0, first=(s == 0))
                with pe.Fori(1, GROUPS // 2 - 1) as k:
                    for s in range(4):
                        unit(4 * k + s, s, k)
                for s in range(4):
                    unit(UNITS - 4 + s, s, GROUPS // 2 - 1, left=(9, 9, 2, 1)[s])
                weigh(UNITS - 1, 3, CHUNKS - 1)
                logits(1, 0)
                o_transpose(UNITS - 1)
                logits(1, 1)

                out_transpose(QUADS - 1)
                project_out(QUADS - 1)
                logits(1, 2)

            ffn(0)
            attention()
            ffn(1)


_ORDER = ["x", "w_qkv_v", "w_qkv_ut", "w_o_v", "w_o_ut", "gate_w", "sh_gate", "sh_up", "sh_down", "r_gate", "r_up", "r_down"]


def kernel(L0_attn_x, L0_attn_W_qkv_v, L0_attn_W_qkv_u, L0_attn_W_o_v, L0_attn_W_o_u, L0_ffn_gate_w,
           L0_ffn_shared_gate_w, L0_ffn_shared_up_w, L0_ffn_shared_down_w, L0_ffn_routed_gate_w,
           L0_ffn_routed_up_w, L0_ffn_routed_down_w):
    import numpy as np
    import concourse.bacc as bacc
    from concourse.bass_utils import run_bass_kernel_spmd

    arrays = [L0_attn_x, L0_attn_W_qkv_v, np.asarray(L0_attn_W_qkv_u).T, L0_attn_W_o_v, np.asarray(L0_attn_W_o_u).T,
              L0_ffn_gate_w, L0_ffn_shared_gate_w, L0_ffn_shared_up_w, L0_ffn_shared_down_w, L0_ffn_routed_gate_w,
              L0_ffn_routed_up_w, L0_ffn_routed_down_w]
    nc = bacc.Bacc("TRN2", target_bir_lowering=False, num_devices=1)
    given, args = {}, []
    for name, a in zip(_ORDER, arrays):
        a = np.ascontiguousarray(a)
        given[f"in_{name}"] = a
        args.append(nc.dram_tensor(f"in_{name}", a.shape, mybir.dt.from_np(a.dtype), kind="ExternalInput").ap())
    out = nc.dram_tensor("out", given["in_x"].shape, F32, kind="ExternalOutput").ap()
    build(nc, *args, out)
    return run_bass_kernel_spmd(nc, [given], core_ids=[0]).results[0]["out"]
```
